# Optimizing a Trainium2 kernel written in Bass

```python
import numpy as np
import jax
import jax.numpy as jnp

def _softmax(x, axis=-1):
    return jax.nn.softmax(x, axis=axis)

def _gelu(x):
    return jax.nn.gelu(x, approximate=True)

def _silu(x):
    return jax.nn.silu(x)

def _sigmoid(x):
    return jax.nn.sigmoid(x)

def _layernorm(x, axis=-1, eps=1e-05):
    m = jnp.mean(x, axis=axis, keepdims=True)
    v = jnp.var(x, axis=axis, keepdims=True)
    return (x - m) / jnp.sqrt(v + eps)

def _scatter_add(tgt, idx, src, axis=0):
    return tgt.at[idx].add(src)

def _segment_sum(src, seg, n):
    return jax.ops.segment_sum(src, seg, n)
kernel_name = 'mk_hybrid_d1_jaxref_r8_07a818'

def setup_inputs(seed: int=0):
    np.random.seed(seed)
    _w = jnp.asarray

    def _L0_attn_a_setup():
        import jax, jax.numpy as jnp
        import numpy as np
        B_, L_, D_MODEL = (4, 256, 128)
        EXPAND = 2
        D_INNER = EXPAND * D_MODEL
        D_STATE = 16
        D_CONV = 4
        DT_RANK = D_MODEL // 16
        A_MIN, A_MAX = (0.0, 1.0)

        def _bound(x):
            return jnp.clip(x, A_MIN, A_MAX)

        def _mamba_forward(hidden_states, W_in, conv_w, conv_b, W_x, W_dt, b_dt, W_out, A_log, D):
            b, l, d = hidden_states.shape
            xz = _bound(jnp.einsum('bld,ed->ble', hidden_states, W_in))
            x, z = jnp.split(xz, 2, axis=-1)
            xc = jnp.transpose(x, (0, 2, 1))
            xc = jax.lax.conv_general_dilated(xc, conv_w, window_strides=(1,), padding=[(D_CONV - 1, 0)], feature_group_count=D_INNER, dimension_numbers=('NCH', 'OIH', 'NCH'))
            xc = xc + conv_b[None, :, None]
            x = _bound(jax.nn.silu(jnp.transpose(xc, (0, 2, 1))))
            x_dbl = jnp.einsum('bld,ed->ble', x, W_x)
            dt = _bound(x_dbl[..., :DT_RANK])
            Bm = x_dbl[..., DT_RANK:DT_RANK + D_STATE]
            Cm = x_dbl[..., DT_RANK + D_STATE:]
            dt = jnp.einsum('blr,dr->bld', dt, W_dt) + b_dt
            dt = jnp.clip(jax.nn.softplus(dt), 0.0001, 20.0)
            A = jnp.exp(A_log)

            def step(h, inp):
                u_t, dt_t, B_t, C_t = inp
                dA = jnp.exp(-dt_t[..., None] * A)
                h = dA * h + (dt_t * u_t)[..., None] * B_t[:, None, :]
                y = jnp.einsum('bdn,bn->bd', h, C_t)
                return (h, y)
            h0 = jnp.zeros((b, D_INNER, D_STATE), dtype=x.dtype)
            xs = (jnp.transpose(x, (1, 0, 2)), jnp.transpose(dt, (1, 0, 2)), jnp.transpose(Bm, (1, 0, 2)), jnp.transpose(Cm, (1, 0, 2)))
            _, ys = jax.lax.scan(step, h0, xs)
            y = jnp.transpose(ys, (1, 0, 2)) + x * D
            y = _bound(y)
            gate = jax.nn.silu(z)
            y = _bound(y * gate)
            return jnp.einsum('bld,ed->ble', y, W_out)
        key = jax.random.key(seed)
        ks = jax.random.split(key, 10)
        s = lambda n: 1.0 / np.sqrt(n)
        return {'hidden_states': jax.random.uniform(ks[0], (B_, L_, D_MODEL), jnp.float32), 'W_in': jax.random.normal(ks[1], (2 * D_INNER, D_MODEL), jnp.float32) * s(D_MODEL), 'conv_w': jax.random.normal(ks[2], (D_INNER, 1, D_CONV), jnp.float32) * s(D_CONV), 'conv_b': jax.random.normal(ks[3], (D_INNER,), jnp.float32) * 0.01, 'W_x': jax.random.normal(ks[4], (DT_RANK + 2 * D_STATE, D_INNER), jnp.float32) * s(D_INNER), 'W_dt': jax.random.normal(ks[5], (D_INNER, DT_RANK), jnp.float32) * s(DT_RANK), 'b_dt': jax.random.normal(ks[6], (D_INNER,), jnp.float32) * 0.01, 'W_out': jax.random.normal(ks[7], (D_MODEL, D_INNER), jnp.float32) * s(D_INNER), 'A_log': jnp.log(jnp.tile(jnp.arange(1, D_STATE + 1, dtype=jnp.float32), (D_INNER, 1))), 'D': jax.random.normal(ks[8], (D_INNER,), jnp.float32)}
    _L0_attn_a_in = _L0_attn_a_setup()

    def _L0_attn_b_setup():
        import jax, jax.numpy as jnp
        import numpy as np
        B, N, DIM = (2, 256, 128)
        H, DH = (16, 64)
        M = 16
        TOPK = 64
        SCALE = DH ** (-0.5)
        key = jax.random.key(seed)
        ks = jax.random.split(key, 8)
        w = 0.02
        return {'x': jax.random.normal(ks[0], (B, N, DIM), jnp.float32), 'Wq': jax.random.normal(ks[1], (DIM, H * DH), jnp.float32) * w, 'Wkv': jax.random.normal(ks[2], (DIM, 2 * H * DH), jnp.float32) * w, 'pre_proj': jax.random.normal(ks[3], (H, H), jnp.float32), 'mem_k': jax.random.normal(ks[4], (H, M, DH), jnp.float32), 'mem_v': jax.random.normal(ks[5], (H, M, DH), jnp.float32), 'Wout': jax.random.normal(ks[6], (H * DH, DIM), jnp.float32) * w, 'bout': jax.random.normal(ks[7], (DIM,), jnp.float32) * w}
    _L0_attn_b_in = _L0_attn_b_setup()

    def _L0_ffn_setup():
        import jax, jax.numpy as jnp
        import numpy as np
        DIM = 128
        DEPTH = 6
        HEADS = 16
        DIM_HEAD = 64
        WINDOW = 32
        INNER = HEADS * DIM_HEAD
        DIM_INNER = int(DIM * 4 * 2 / 3)
        QK_SCALE = 8.0

        def shift_tokens(t):
            a, s = jnp.split(t, 2, -1)
            s = jnp.pad(s, ((0, 0), (1, 0), (0, 0)))[:, :-1]
            return jnp.concatenate([a, s], -1)

        def l2norm(t):
            return t / jnp.maximum(jnp.linalg.norm(t, axis=-1, keepdims=True), 1e-12)

        def rotate_half(x):
            x1, x2 = jnp.split(x, 2, -1)
            return jnp.concatenate([-x2, x1], -1)

        def rotary_tables(n):
            half = jnp.arange(0, DIM_HEAD, 2, dtype=jnp.float32)
            inv_freq = 1.0 / 10000.0 ** (half / DIM_HEAD)
            t = jnp.arange(n, dtype=jnp.float32)
            freqs = t[:, None] * inv_freq[None, :]
            freqs = jnp.concatenate([freqs, freqs], -1)
            base_scale = (half + 0.4 * DIM_HEAD) / (1.4 * DIM_HEAD)
            power = (t - n // 2) / (WINDOW // 2)
            scale = base_scale[None, :] ** power[:, None]
            scale = jnp.concatenate([scale, scale], -1)
            return (freqs, scale)

        def local_attention(q, k, v):
            b, h, n, d = q.shape
            w = WINDOW
            nw = n // w
            bq = q.reshape(b, h, nw, w, d)
            bk = k.reshape(b, h, nw, w, d)
            bv = v.reshape(b, h, nw, w, d)

            def look(t):
                p = jnp.pad(t, ((0, 0), (0, 0), (1, 0), (0, 0), (0, 0)))
                return jnp.concatenate([p[:, :, :nw], p[:, :, 1:]], axis=3)
            bk2, bv2 = (look(bk), look(bv))
            seq = jnp.arange(n).reshape(nw, w)
            seq_p = jnp.pad(seq, ((1, 0), (0, 0)), constant_values=-1)
            jt = jnp.concatenate([seq_p[:nw], seq_p[1:]], axis=1)
            it = seq[:, :, None]
            jb = jt[:, None, :]
            mask = (it < jb) | (it > jb + w) | (jb == -1)
            sim = jnp.einsum('bhwie,bhwje->bhwij', bq, bk2) * QK_SCALE
            sim = jnp.where(mask, -jnp.finfo(sim.dtype).max, sim)
            attn = jax.nn.softmax(sim, -1)
            out = jnp.einsum('bhwij,bhwje->bhwie', attn, bv2)
            return out.reshape(b, h, n, d)

        def attn_layer(x, Wqkv, qs, ksc, Wo):
            b, n, _ = x.shape
            qkv = x @ Wqkv
            q, k, v = jnp.split(qkv, 3, -1)
            sh = lambda t: t.reshape(b, n, HEADS, DIM_HEAD).transpose(0, 2, 1, 3)
            q, k, v = (sh(q), sh(k), sh(v))
            q = l2norm(q) * qs
            k = l2norm(k) * ksc
            freqs, scale = rotary_tables(n)
            cos, sin = (jnp.cos(freqs), jnp.sin(freqs))
            q = q * cos * scale + rotate_half(q) * sin * scale
            inv = 1.0 / scale
            k = k * cos * inv + rotate_half(k) * sin * inv
            out = local_attention(q, k, v)
            out = out.transpose(0, 2, 1, 3).reshape(b, n, INNER)
            return out @ Wo

        def ffn_layer(x, g, bln, W1, b1, W2, b2):
            mu = x.mean(-1, keepdims=True)
            var = ((x - mu) ** 2).mean(-1, keepdims=True)
            xn = (x - mu) / jnp.sqrt(var + 1e-05) * g + bln
            hg = xn @ W1 + b1
            a, gate = jnp.split(hg, 2, -1)
            return a * jax.nn.gelu(gate, approximate=False) @ W2 + b2
        key = jax.random.key(seed)
        ks = jax.random.split(key, 8)
        B, N = (2, 256)
        init = lambda k, shape: jax.random.normal(k, shape, jnp.float32) * 0.02
        return {'x': jax.random.normal(ks[0], (B, N, DIM), jnp.float32), 'Wqkv': init(ks[1], (DEPTH, DIM, 3 * INNER)), 'q_scale': jnp.ones((DEPTH, DIM_HEAD), jnp.float32), 'k_scale': jnp.ones((DEPTH, DIM_HEAD), jnp.float32), 'Wo': init(ks[2], (DEPTH, INNER, DIM)), 'ln_g': jnp.ones((DEPTH, DIM), jnp.float32), 'ln_b': jnp.zeros((DEPTH, DIM), jnp.float32), 'W1': init(ks[3], (DEPTH, DIM, 2 * DIM_INNER)), 'b1': jnp.zeros((DEPTH, 2 * DIM_INNER), jnp.float32), 'W2': init(ks[4], (DEPTH, DIM_INNER, DIM)), 'b2': jnp.zeros((DEPTH, DIM), jnp.float32)}
    _L0_ffn_in = _L0_ffn_setup()
    _d = {'L0_attn_a_hidden_states': _L0_attn_a_in['hidden_states'], 'L0_attn_a_W_in': _L0_attn_a_in['W_in'], 'L0_attn_a_conv_w': _L0_attn_a_in['conv_w'], 'L0_attn_a_conv_b': _L0_attn_a_in['conv_b'], 'L0_attn_a_W_x': _L0_attn_a_in['W_x'], 'L0_attn_a_W_dt': _L0_attn_a_in['W_dt'], 'L0_attn_a_b_dt': _L0_attn_a_in['b_dt'], 'L0_attn_a_W_out': _L0_attn_a_in['W_out'], 'L0_attn_a_A_log': _L0_attn_a_in['A_log'], 'L0_attn_a_D': _L0_attn_a_in['D'], 'L0_attn_b_Wq': _L0_attn_b_in['Wq'], 'L0_attn_b_Wkv': _L0_attn_b_in['Wkv'], 'L0_attn_b_pre_proj': _L0_attn_b_in['pre_proj'], 'L0_attn_b_mem_k': _L0_attn_b_in['mem_k'], 'L0_attn_b_mem_v': _L0_attn_b_in['mem_v'], 'L0_attn_b_Wout': _L0_attn_b_in['Wout'], 'L0_attn_b_bout': _L0_attn_b_in['bout'], 'L0_ffn_Wqkv': _L0_ffn_in['Wqkv'], 'L0_ffn_q_scale': _L0_ffn_in['q_scale'], 'L0_ffn_k_scale': _L0_ffn_in['k_scale'], 'L0_ffn_Wo': _L0_ffn_in['Wo'], 'L0_ffn_ln_g': _L0_ffn_in['ln_g'], 'L0_ffn_ln_b': _L0_ffn_in['ln_b'], 'L0_ffn_W1': _L0_ffn_in['W1'], 'L0_ffn_b1': _L0_ffn_in['b1'], 'L0_ffn_W2': _L0_ffn_in['W2'], 'L0_ffn_b2': _L0_ffn_in['b2']}
    _x0 = _d['L0_attn_a_hidden_states']
    _d['L0_attn_a_hidden_states'] = jax.random.normal(jax.random.fold_in(jax.random.key(seed), 1), (4, 512, 128), dtype=_x0.dtype)
    del _x0
    return _d

def reference(L0_attn_a_hidden_states, L0_attn_a_W_in, L0_attn_a_conv_w, L0_attn_a_conv_b, L0_attn_a_W_x, L0_attn_a_W_dt, L0_attn_a_b_dt, L0_attn_a_W_out, L0_attn_a_A_log, L0_attn_a_D, L0_attn_b_Wq, L0_attn_b_Wkv, L0_attn_b_pre_proj, L0_attn_b_mem_k, L0_attn_b_mem_v, L0_attn_b_Wout, L0_attn_b_bout, L0_ffn_Wqkv, L0_ffn_q_scale, L0_ffn_k_scale, L0_ffn_Wo, L0_ffn_ln_g, L0_ffn_ln_b, L0_ffn_W1, L0_ffn_b1, L0_ffn_W2, L0_ffn_b2):

    def _L0_attn_a_ref(hidden_states, W_in, conv_w, conv_b, W_x, W_dt, b_dt, W_out, A_log, D):
        import jax, jax.numpy as jnp
        import numpy as np
        B_, L_, D_MODEL = (4, 256, 128)
        EXPAND = 2
        D_INNER = EXPAND * D_MODEL
        D_STATE = 16
        D_CONV = 4
        DT_RANK = D_MODEL // 16
        A_MIN, A_MAX = (0.0, 1.0)

        def _bound(x):
            return jnp.clip(x, A_MIN, A_MAX)

        def _mamba_forward(hidden_states, W_in, conv_w, conv_b, W_x, W_dt, b_dt, W_out, A_log, D):
            b, l, d = hidden_states.shape
            xz = _bound(jnp.einsum('bld,ed->ble', hidden_states, W_in))
            x, z = jnp.split(xz, 2, axis=-1)
            xc = jnp.transpose(x, (0, 2, 1))
            xc = jax.lax.conv_general_dilated(xc, conv_w, window_strides=(1,), padding=[(D_CONV - 1, 0)], feature_group_count=D_INNER, dimension_numbers=('NCH', 'OIH', 'NCH'))
            xc = xc + conv_b[None, :, None]
            x = _bound(jax.nn.silu(jnp.transpose(xc, (0, 2, 1))))
            x_dbl = jnp.einsum('bld,ed->ble', x, W_x)
            dt = _bound(x_dbl[..., :DT_RANK])
            Bm = x_dbl[..., DT_RANK:DT_RANK + D_STATE]
            Cm = x_dbl[..., DT_RANK + D_STATE:]
            dt = jnp.einsum('blr,dr->bld', dt, W_dt) + b_dt
            dt = jnp.clip(jax.nn.softplus(dt), 0.0001, 20.0)
            A = jnp.exp(A_log)

            def step(h, inp):
                u_t, dt_t, B_t, C_t = inp
                dA = jnp.exp(-dt_t[..., None] * A)
                h = dA * h + (dt_t * u_t)[..., None] * B_t[:, None, :]
                y = jnp.einsum('bdn,bn->bd', h, C_t)
                return (h, y)
            h0 = jnp.zeros((b, D_INNER, D_STATE), dtype=x.dtype)
            xs = (jnp.transpose(x, (1, 0, 2)), jnp.transpose(dt, (1, 0, 2)), jnp.transpose(Bm, (1, 0, 2)), jnp.transpose(Cm, (1, 0, 2)))
            _, ys = jax.lax.scan(step, h0, xs)
            y = jnp.transpose(ys, (1, 0, 2)) + x * D
            y = _bound(y)
            gate = jax.nn.silu(z)
            y = _bound(y * gate)
            return jnp.einsum('bld,ed->ble', y, W_out)
        return _mamba_forward(hidden_states, W_in, conv_w, conv_b, W_x, W_dt, b_dt, W_out, A_log, D)

    def _L0_attn_b_ref(x, Wq, Wkv, pre_proj, mem_k, mem_v, Wout, bout):
        import jax, jax.numpy as jnp
        import numpy as np
        B, N, DIM = (2, 256, 128)
        H, DH = (16, 64)
        M = 16
        TOPK = 64
        SCALE = DH ** (-0.5)
        b, n, _ = x.shape
        q = (x @ Wq).reshape(b, n, H, DH).transpose(0, 2, 1, 3)
        kv = x @ Wkv
        k = kv[..., :H * DH].reshape(b, n, H, DH).transpose(0, 2, 1, 3)
        v = kv[..., H * DH:].reshape(b, n, H, DH).transpose(0, 2, 1, 3)
        k = jnp.concatenate([jnp.broadcast_to(mem_k, (b, H, M, DH)), k], axis=2)
        v = jnp.concatenate([jnp.broadcast_to(mem_v, (b, H, M, DH)), v], axis=2)
        j = n + M
        dots = jnp.einsum('bhid,bhjd->bhij', q, k) * SCALE
        dots = jnp.einsum('bhij,hk->bkij', dots, pre_proj)
        mask_value = -jnp.finfo(dots.dtype).max
        causal = jnp.triu(jnp.ones((n, j), bool), j - n + 1)
        dots = jnp.where(causal, mask_value, dots)
        kth = jax.lax.top_k(dots, TOPK)[0][..., -1:]
        dots = jnp.where(dots < kth, mask_value, dots)
        attn = jax.nn.softmax(dots, axis=-1)
        out = jnp.einsum('bhij,bhjd->bhid', attn, v)
        out = out.transpose(0, 2, 1, 3).reshape(b, n, H * DH)
        return out @ Wout + bout

    def _L0_ffn_ref(x, Wqkv, q_scale, k_scale, Wo, ln_g, ln_b, W1, b1, W2, b2):
        import jax, jax.numpy as jnp
        import numpy as np
        DIM = 128
        DEPTH = 6
        HEADS = 16
        DIM_HEAD = 64
        WINDOW = 32
        INNER = HEADS * DIM_HEAD
        DIM_INNER = int(DIM * 4 * 2 / 3)
        QK_SCALE = 8.0

        def shift_tokens(t):
            a, s = jnp.split(t, 2, -1)
            s = jnp.pad(s, ((0, 0), (1, 0), (0, 0)))[:, :-1]
            return jnp.concatenate([a, s], -1)

        def l2norm(t):
            return t / jnp.maximum(jnp.linalg.norm(t, axis=-1, keepdims=True), 1e-12)

        def rotate_half(x):
            x1, x2 = jnp.split(x, 2, -1)
            return jnp.concatenate([-x2, x1], -1)

        def rotary_tables(n):
            half = jnp.arange(0, DIM_HEAD, 2, dtype=jnp.float32)
            inv_freq = 1.0 / 10000.0 ** (half / DIM_HEAD)
            t = jnp.arange(n, dtype=jnp.float32)
            freqs = t[:, None] * inv_freq[None, :]
            freqs = jnp.concatenate([freqs, freqs], -1)
            base_scale = (half + 0.4 * DIM_HEAD) / (1.4 * DIM_HEAD)
            power = (t - n // 2) / (WINDOW // 2)
            scale = base_scale[None, :] ** power[:, None]
            scale = jnp.concatenate([scale, scale], -1)
            return (freqs, scale)

        def local_attention(q, k, v):
            b, h, n, d = q.shape
            w = WINDOW
            nw = n // w
            bq = q.reshape(b, h, nw, w, d)
            bk = k.reshape(b, h, nw, w, d)
            bv = v.reshape(b, h, nw, w, d)

            def look(t):
                p = jnp.pad(t, ((0, 0), (0, 0), (1, 0), (0, 0), (0, 0)))
                return jnp.concatenate([p[:, :, :nw], p[:, :, 1:]], axis=3)
            bk2, bv2 = (look(bk), look(bv))
            seq = jnp.arange(n).reshape(nw, w)
            seq_p = jnp.pad(seq, ((1, 0), (0, 0)), constant_values=-1)
            jt = jnp.concatenate([seq_p[:nw], seq_p[1:]], axis=1)
            it = seq[:, :, None]
            jb = jt[:, None, :]
            mask = (it < jb) | (it > jb + w) | (jb == -1)
            sim = jnp.einsum('bhwie,bhwje->bhwij', bq, bk2) * QK_SCALE
            sim = jnp.where(mask, -jnp.finfo(sim.dtype).max, sim)
            attn = jax.nn.softmax(sim, -1)
            out = jnp.einsum('bhwij,bhwje->bhwie', attn, bv2)
            return out.reshape(b, h, n, d)

        def attn_layer(x, Wqkv, qs, ksc, Wo):
            b, n, _ = x.shape
            qkv = x @ Wqkv
            q, k, v = jnp.split(qkv, 3, -1)
            sh = lambda t: t.reshape(b, n, HEADS, DIM_HEAD).transpose(0, 2, 1, 3)
            q, k, v = (sh(q), sh(k), sh(v))
            q = l2norm(q) * qs
            k = l2norm(k) * ksc
            freqs, scale = rotary_tables(n)
            cos, sin = (jnp.cos(freqs), jnp.sin(freqs))
            q = q * cos * scale + rotate_half(q) * sin * scale
            inv = 1.0 / scale
            k = k * cos * inv + rotate_half(k) * sin * inv
            out = local_attention(q, k, v)
            out = out.transpose(0, 2, 1, 3).reshape(b, n, INNER)
            return out @ Wo

        def ffn_layer(x, g, bln, W1, b1, W2, b2):
            mu = x.mean(-1, keepdims=True)
            var = ((x - mu) ** 2).mean(-1, keepdims=True)
            xn = (x - mu) / jnp.sqrt(var + 1e-05) * g + bln
            hg = xn @ W1 + b1
            a, gate = jnp.split(hg, 2, -1)
            return a * jax.nn.gelu(gate, approximate=False) @ W2 + b2
        for i in range(DEPTH):
            x = attn_layer(shift_tokens(x), Wqkv[i], q_scale[i], k_scale[i], Wo[i]) + x
            x = ffn_layer(shift_tokens(x), ln_g[i], ln_b[i], W1[i], b1[i], W2[i], b2[i]) + x
        return x
    x = L0_attn_a_hidden_states
    x = x + _L0_attn_a_ref(_layernorm(x, axis=-1), L0_attn_a_W_in, L0_attn_a_conv_w, L0_attn_a_conv_b, L0_attn_a_W_x, L0_attn_a_W_dt, L0_attn_a_b_dt, L0_attn_a_W_out, L0_attn_a_A_log, L0_attn_a_D)
    x = x + _L0_ffn_ref(_layernorm(x, axis=-1), L0_ffn_Wqkv, L0_ffn_q_scale, L0_ffn_k_scale, L0_ffn_Wo, L0_ffn_ln_g, L0_ffn_ln_b, L0_ffn_W1, L0_ffn_b1, L0_ffn_W2, L0_ffn_b2)
    x = x + _L0_attn_b_ref(_layernorm(x, axis=-1), L0_attn_b_Wq, L0_attn_b_Wkv, L0_attn_b_pre_proj, L0_attn_b_mem_k, L0_attn_b_mem_v, L0_attn_b_Wout, L0_attn_b_bout)
    x = x + _L0_ffn_ref(_layernorm(x, axis=-1), L0_ffn_Wqkv, L0_ffn_q_scale, L0_ffn_k_scale, L0_ffn_Wo, L0_ffn_ln_g, L0_ffn_ln_b, L0_ffn_W1, L0_ffn_b1, L0_ffn_W2, L0_ffn_b2)
    return x

_drawn_inputs = setup_inputs


def setup_inputs(seed=0):
    import zlib

    import numpy as np

    out = dict(_drawn_inputs(seed))
    spreads = {'L0_ffn_q_scale': (1.0, 0.6),
     'L0_ffn_k_scale': (1.0, 0.6),
     'L0_ffn_ln_g': (1.0, 0.6),
     'L0_ffn_ln_b': (0.0, 0.8),
     'L0_ffn_b1': (0.0, 0.576),
     'L0_ffn_b2': (0.0, 0.1)}
    factors = {'L0_attn_a_conv_b': 8.0,
     'L0_attn_a_W_x': 3.422,
     'L0_attn_a_W_dt': 8.0,
     'L0_attn_a_b_dt': 200.0,
     'L0_attn_a_A_log': 69.956,
     'L0_attn_b_Wkv': 4.805,
     'L0_attn_b_bout': 5.454,
     'L0_attn_b_mem_k': 3.98,
     'L0_attn_b_mem_v': 3.0}
    for name, (base, spread) in spreads.items():
        noise = np.random.default_rng([zlib.crc32(name.encode()), seed]).standard_normal(out[name].shape)
        drawn = base * np.exp(spread * noise) if base else spread * noise
        out[name] = jnp.asarray(drawn.astype(out[name].dtype))
    for name, factor in factors.items():
        out[name] = (out[name] * factor).astype(out[name].dtype)
    return out
```

```python
from contextlib import ExitStack

import concourse.bass as bass
import numpy as np
from concourse import mybir

ALU = mybir.AluOpType
ACT = mybir.ActivationFunctionType
AX_X = mybir.AxisListType.X
F32 = mybir.dt.float32
BF16 = mybir.dt.bfloat16
U32 = mybir.dt.uint32
ds = bass.ds

P = 128
B, N, D = 4, 512, 128
H, DH = 16, 64
INNER = H * DH
WIN = 32
DEPTH = LAYERS = 6
HID = 341
PAD = WIN + 1
ROW = PAD + N
TILES = N // P
LT = B * TILES
PAIRS = H // 2
WPT = P // WIN
QK_SCALE = 8.0
EPS = 1e-5
MEM = 16
TOPK = 64
DI, DS, DC, DR = 256, 16, 4, 8
CI = DI // P
XD = DR + 2 * DS
MASKED = -3.0e38
REMOVED = -3.4e38
MAGIC = 0x5F3759DF
NEWTON = 11
HCH = [(0, 128), (128, 128), (256, 85)]


def rotary_tables():
    half = np.arange(0, DH, 2, dtype=np.float32)
    inv_freq = (np.float32(1.0) / np.float32(10000.0) ** (half / np.float32(DH))).astype(np.float32)
    t = np.arange(N, dtype=np.float32)
    freqs = t[:, None] * inv_freq[None, :]
    freqs = np.concatenate([freqs, freqs], -1)
    base = (half + np.float32(0.4 * DH)) / np.float32(1.4 * DH)
    power = (t - N // 2) / np.float32(WIN // 2)
    scale = base[None, :] ** power[:, None]
    scale = np.concatenate([scale, scale], -1).astype(np.float32)
    cos, sin = np.cos(freqs), np.sin(freqs)
    sign = np.where(np.arange(DH) < DH // 2, -1.0, 1.0).astype(np.float32)[None, :]
    inv = np.float32(1.0) / scale
    return np.stack([cos * scale * QK_SCALE, cos * inv, sign * sin * scale * QK_SCALE, sign * sin * inv]).astype(np.float32)


class Kit:
    pass


def names(ctx, phase, nc, *which):
    made = {w: ctx.enter_context(nc.semaphore(f"{phase}_{w}")) for w in which}
    with nc.Block() as block:
        @block.sync
        def _(sp):
            for sem in made.values():
                sp.sem_inc(sem, 1)

    def clear():
        with nc.Block() as block:
            @block.sync
            def _(sp):
                for sem in made.values():
                    sp.sem_clear(sem)

    ctx.callback(clear)
    return made


def wait_alone(eng, sem, value, scrap):
    eng.wait_ge(sem, 1 + value)
    eng.sem_inc(scrap, 1)



LN_SEMS = ("ln_mean", "ln_centred", "ln_squared", "ln_var", "ln_sd", "ln_recip", "ln_done")


def ln_tensor(pe, k, s, src, base, ready):
    for b in range(B):
        ready(b)
        if b >= 2:
            pe.wait_ge(s["ln_centred"], 1 + base + b - 1)
        pe.matmul(k.psum[:, b % 2, :], k.mean_w[:, :], src(b), start=True, stop=True).then_inc(s["ln_mean"], 1)
        if b >= 1:
            var(pe, k, s, b - 1, base)
    var(pe, k, s, B - 1, base)


def var(pe, k, s, b, base):
    pe.wait_ge(s["ln_squared"], 1 + base + b + 1)
    if b >= 2:
        pe.wait_ge(s["ln_sd"], 1 + base + b - 1)
    pe.matmul(k.psum[:, 2 + b % 2, :], k.mean_w[:, :], k.ln_sq[:, b % 2, :], start=True, stop=True).then_inc(s["ln_var"], 1)


def ln_scalar(act, k, s, dst, base):
    for b in range(B + 1):
        if b < B:
            act.wait_ge(s["ln_centred"], 1 + base + b + 1)
            if b >= 2:
                act.wait_ge(s["ln_var"], 1 + base + b - 1)
            act.activation(k.ln_sq[:, b % 2, :], dst(b), ACT.Square).then_inc(s["ln_squared"], 1)
        if b >= 1:
            act.wait_ge(s["ln_var"], 1 + base + b)
            if b >= 3:
                act.wait_ge(s["ln_done"], 1 + base + b - 2)
            act.activation(k.ln_std[:, (b - 1) % 2, :], k.psum[:, 2 + (b - 1) % 2, :], ACT.Sqrt,
                           bias=k.eps[:, 0:1]).then_inc(s["ln_sd"], 1)


def ln_vector(dve, k, s, src, dst, base, gain=None, shift=None):
    for b in range(B + 1):
        if b < B:
            dve.wait_ge(s["ln_mean"], 1 + base + b + 1)
            dve.tensor_tensor(dst(b), src(b), k.psum[:, b % 2, :], ALU.subtract).then_inc(s["ln_centred"], 1)
        if b >= 1:
            std = k.ln_std[:, (b - 1) % 2, :]
            dve.wait_ge(s["ln_sd"], 1 + base + b)
            dve.reciprocal(std, std).then_inc(s["ln_recip"], 1)
            steps = 1 if gain is None else 2
            dve.wait_ge(s["ln_recip"], 1 + steps * base + steps * (b - 1) + 1)
            if gain is None:
                dve.tensor_tensor(dst(b - 1), dst(b - 1), std, ALU.mult).then_inc(s["ln_done"], 1)
            else:
                dve.tensor_tensor(dst(b - 1), dst(b - 1), std, ALU.mult).then_inc(s["ln_recip"], 1)
                dve.wait_ge(s["ln_recip"], 1 + steps * base + steps * b)
                dve.tensor_scalar(dst(b - 1), dst(b - 1), gain, shift, ALU.mult, ALU.add).then_inc(s["ln_done"], 1)


def norm_phase(k, phase):
    nc = k.nc
    src = lambda b: k.X[:, b, PAD:ROW]
    dst = lambda b: k.XA[:, b, PAD:ROW]
    with ExitStack() as ctx:
        s = names(ctx, phase, nc, *LN_SEMS)
        k.ln_sq = ctx.enter_context(nc.sbuf_tensor(f"{phase}_ln_sq", [P, 2, N], F32))
        k.ln_std = ctx.enter_context(nc.sbuf_tensor(f"{phase}_ln_std", [P, 2, N], F32))
        with nc.Block() as block:
            @block.tensor
            def _(pe):
                ln_tensor(pe, k, s, src, 0, lambda b: None)

            @block.scalar
            def _(act):
                ln_scalar(act, k, s, dst, 0)

            @block.vector
            def _(dve):
                ln_vector(dve, k, s, src, dst, 0)



def load_phase(k, a):
    nc = k.nc
    x_rows = a["x"].rearrange("b (t p) d -> p (b t) d", p=P)
    small = lambda i, m: k.psum[0:m, 4, DEPTH * i:DEPTH * (i + 1)]
    with ExitStack() as ctx:
        s = names(ctx, "load", nc, "x_in", "small_in", "zeroed", "built", "turned", "copied")
        x_tok = ctx.enter_context(nc.sbuf_tensor("x_tok", [P, LT, P], F32))
        b1_rows = ctx.enter_context(nc.sbuf_tensor("b1_rows", [DEPTH, 2 * HID], F32))
        d_rows = ctx.enter_context(nc.sbuf_tensor("d_rows", [DEPTH, 3, D], F32))
        block = ctx.enter_context(nc.Block())

        @block.sync
        def _(sp):
            sp.dma_start(x_tok[:, :, :], x_rows).then_inc(s["x_in"], 16)
            sp.dma_start(b1_rows[:, :], a["b1"]).then_inc(s["small_in"], 16)
            for i, v in enumerate((a["b2"], a["ln_g"], a["ln_b"])):
                sp.dma_start(d_rows[:, i, :], v).then_inc(s["small_in"], 16)
            sp.dma_start(k.rot_base[:, :, :, :], a["rot"].rearrange("c (t p) e -> p c t e", p=P)).then_inc(s["small_in"], 16)
            sp.dma_start(k.qk_gain[:, 0, :, :], a["q_scale"].partition_broadcast(P)).then_inc(s["small_in"], 16)
            sp.dma_start(k.qk_gain[:, 1, :, :], a["k_scale"].partition_broadcast(P)).then_inc(s["small_in"], 16)
            sp.wait_ge(s["small_in"], 1 + 16 * 7)

        @block.gpsimd
        def _(pool):
            pool.memset(k.ident[:, :], 0.0).then_inc(s["zeroed"], 1)
            pool.memset(k.mask_f[:, :], 0.0).then_inc(s["zeroed"], 1)
            pool.wait_ge(s["zeroed"], 1 + 2)
            pool.affine_select(out=k.ident[:, :], in_=k.ident[:, :], compare_op=ALU.not_equal, fill=1.0, base=0,
                               pattern=[[-1, P]], channel_multiplier=1).then_inc(s["built"], 1)
            pool.memset(k.mean_w[:, :], 1.0 / D).then_inc(s["built"], 1)
            pool.memset(k.eps[:, :], EPS).then_inc(s["built"], 1)
            pool.memset(k.one[:, :], 1.0).then_inc(s["built"], 1)
            pool.affine_select(out=k.mask_f[:, 0:P], in_=k.mask_f[:, 0:P], compare_op=ALU.is_ge, fill=MASKED, base=0,
                               pattern=[[-1, P]], channel_multiplier=1).then_inc(s["built"], 1)
            pool.wait_ge(s["built"], 1 + 5)
            pool.tensor_copy(k.ident_bf[:, :], k.ident[:, :]).then_inc(s["built"], 1)
            pool.tensor_copy(k.causal[:, :], k.mask_f[:, 0:P]).then_inc(s["built"], 1)
            band = k.mask_f[:, 0:2 * WIN]
            pool.wait_ge(s["built"], 1 + 7)
            pool.memset(band, 0.0).then_inc(s["built"], 1)
            for w in range(WPT):
                rows = slice(WIN * w, WIN * (w + 1))
                part = k.mask_f[rows, 0:2 * WIN]
                pool.wait_ge(s["built"], 1 + 8 + 2 * w)
                pool.affine_select(out=part, in_=part, compare_op=ALU.is_ge, fill=MASKED, base=0,
                                   pattern=[[1, 2 * WIN]], channel_multiplier=-1).then_inc(s["built"], 1)
                pool.wait_ge(s["built"], 1 + 9 + 2 * w)
                pool.affine_select(out=part, in_=part, compare_op=ALU.is_ge, fill=MASKED, base=WIN,
                                   pattern=[[-1, 2 * WIN]], channel_multiplier=1).then_inc(s["built"], 1)
            for m in range(2):
                if m:
                    pool.wait_ge(s["built"], 1 + 17)
                    pool.memset(k.mask_f[0:WIN, 0:WIN], MASKED).then_inc(s["built"], 1)
                pool.wait_ge(s["built"], 1 + 16 + 2 * m)
                pool.tensor_copy(k.band[:, m, :, :], band.unsqueeze(1).to_broadcast([P, 8, 2 * WIN])).then_inc(s["built"], 1)

        @block.vector
        def _(dve):
            dve.memset(k.XA[:, :, :], 0.0)
            dve.memset(k.XB[:, :, :], 0.0)
            dve.memset(k.magic[:, :], MAGIC + 1)
            for u in range(4):
                dve.wait_ge(s["turned"], 1 + u + 1)
                dve.tensor_copy(k.X[:, u, PAD:ROW], k.psum[:, u, :]).then_inc(s["copied"], 1)
            dve.wait_ge(s["turned"], 1 + 5)
            for which in range(2):
                for c, (h0, m) in enumerate(HCH):
                    dve.tensor_copy(k.b1[0:m, :, which, c], small(which * 3 + c, m))
            for i, t in enumerate((k.b2, k.ln_g, k.ln_b)):
                dve.tensor_copy(t[:, :], small(6 + i, D))

        @block.tensor
        def _(pe):
            pe.wait_ge(s["x_in"], 1 + 16)
            pe.wait_ge(s["built"], 1 + 1)
            for u in range(4):
                for t in range(4):
                    last = pe.transpose(k.psum[:, u, t * P:(t + 1) * P], x_tok[:, 4 * u + t, :], k.ident[:, :])
                last.then_inc(s["turned"], 1)
            pe.wait_ge(s["small_in"], 1 + 16 * 7)
            for which in range(2):
                for c, (h0, m) in enumerate(HCH):
                    pe.transpose(small(which * 3 + c, m), b1_rows[:, which * HID + h0:which * HID + h0 + m], k.ident[0:DEPTH, 0:DEPTH])
            for i in range(3):
                last = pe.transpose(small(6 + i, D), d_rows[:, i, :], k.ident[0:DEPTH, 0:DEPTH])
            last.then_inc(s["turned"], 1)


def store_phase(k, out):
    nc = k.nc
    rows = out.rearrange("b (t p) d -> p b t d", p=P)
    with ExitStack() as ctx:
        s = names(ctx, "store", nc, "turned", "copied", "stored")
        y_tok = ctx.enter_context(nc.sbuf_tensor("y_tok", [P, B, TILES, P], F32))
        block = ctx.enter_context(nc.Block())

        @block.tensor
        def _(pe):
            for b in range(B):
                for t in range(TILES):
                    last = pe.transpose(k.psum[:, b, t * P:(t + 1) * P], k.X[:, b, PAD + t * P:PAD + (t + 1) * P], k.ident[:, :])
                last.then_inc(s["turned"], 1)

        @block.vector
        def _(dve):
            for b in range(B):
                dve.wait_ge(s["turned"], 1 + b + 1)
                dve.tensor_copy(y_tok[:, b, :, :], k.psum[:, b, :].rearrange("p (t d) -> p t d", t=TILES)).then_inc(s["copied"], 1)

        @block.sync
        def _(sp):
            for b in range(B):
                sp.wait_ge(s["copied"], 1 + b + 1)
                sp.dma_start(rows[:, b, :, :], y_tok[:, b, :, :]).then_inc(s["stored"], 16)
            sp.wait_ge(s["stored"], 1 + 16 * B)


def add_phase(k, phase):
    with k.nc.Block() as block:
        @block.vector
        def _(dve):
            for b in range(B):
                dve.tensor_tensor(k.X[:, b, PAD:ROW], k.X[:, b, PAD:ROW], k.XA[:, b, PAD:ROW], ALU.add)



def turn_units(kk):
    if isinstance(kk, int):
        return sum((3 <= j <= 18) + 4 * (1 <= j <= 16) + 4 * (2 <= j <= 17) for j in range(kk))
    return 9 * kk - 15


TURN_LAYER = 9 * LT


def ffn_stack(k, a, phase):
    nc = k.nc
    with ExitStack() as ctx:
        s = names(ctx, phase, nc, *LN_SEMS, "wqkv_in", "wo_in", "w12_in", "tabled", "zeroed", "xs_ready", "proj_full", "proj_evac",
                  "sq_done", "ss_done", "newton", "rn_ready", "norm_done", "rot_done", "add_done", "t_full",
                  "t_evac", "scores", "top", "sub_done", "exp_done", "summed", "rden_done", "pv_done", "on_done",
                  "wo_done", "res_done", "shifted", "gate_full", "gate_evac", "val_full", "val_evac", "out_full", "out_evac", "scrap")

        def sb(name, shape, dt=F32):
            return ctx.enter_context(nc.sbuf_tensor(f"{phase}_{name}", shape, dt))

        wqkv = sb("wqkv", [P, 3 * INNER])
        wo = sb("wo", [P, PAIRS, D])
        w1 = sb("w1", [P, 2 * HID])
        w2 = sb("w2", [P, 3, D])
        rot = sb("rot", [P, 4, TILES, DH])
        xs = sb("xs", [P, 2, WIN + P])
        raw = sb("raw", [P, 2, H, DH])
        sq = sb("sq", [P, 2, H, DH])
        ss = sb("ss", [P, 2 * H])
        nt = sb("nt", [P, 4, 2 * H])
        rn = sb("rn", [P, 2 * H])
        rope = sb("rope", [P, 2, 2, H, DH])
        t2 = sb("t2", [P, 2, H, DH])
        qT = sb("qT", [P, PAIRS, P])
        kT = sb("kT", [P, PAIRS, 2, WIN + 2 * P])
        v2 = sb("v2", [P, 2, WPT, PAIRS, 2, DH])
        prob = sb("prob", [P, H, 2 * WIN])
        probT = sb("probT", [P, PAIRS, P])
        top = sb("top", [P, H])
        den = sb("den", [P, H])
        rden = sb("rden", [P, 2, H])
        o_tok = sb("o_tok", [P, H, DH])
        oT = sb("oT", [P, PAIRS, P])
        wo_sb = sb("wo_sb", [P, P])
        xn = raw[:, :, :, :].rearrange("p a h e -> p (a h e)").rearrange("p (b n) -> p b n", b=B)
        k.ln_sq = sq[:, 0, :, :].rearrange("p h e -> p (h e)").rearrange("p (i n) -> p i n", i=2)
        k.ln_std = sq[:, 1, :, :].rearrange("p h e -> p (h e)").rearrange("p (i n) -> p i n", i=2)
        gate = t2[:, 0, :, :].rearrange("p h e -> p (h e)").rearrange("p (i n) -> p i n", i=2)
        hid = rope[:, :, :, :, :].rearrange("p a c h e -> p (a c h e)").rearrange("p (i c n) -> p i c n", i=2, c=4)

        psum = k.psum

        def steps(eng, fn, L):
            for j in range(4):
                fn(L, 0, j, j)
            with eng.Fori(1, B) as b:
                for j in range(4):
                    fn(L, b, j, 4 * b + j)
            for j in range(3):
                fn(L, B, j, LT + j)

        def tile(x, r0, r1, b, t0, n=WIN + P):
            if isinstance(b, int):
                return x[r0:r1, b, t0:t0 + n]
            return x[r0:r1, ds(b, 1), t0:t0 + n].rearrange("p o n -> p (o n)")

        def on(kk, lag):
            return not isinstance(kk, int) or 0 <= kk - lag < LT

        with nc.Block() as block:
            @block.sync
            def _(sp):
                with sp.Fori(0, LAYERS) as L:
                    sp.wait_ge(s["proj_evac"], 1 + 8 * LT * L + 2)
                    sp.dma_start(wqkv[:, :], a["Wqkv"][ds(L, 1), :, :].rearrange("l p n -> p (l n)")).then_inc(s["wqkv_in"], 16)
                    sp.wait_ge(s["wo_done"], 1 + LT * L + 1)
                    sp.dma_start(wo[:, :, :], a["Wo"][ds(L, 1), :, :].rearrange("l (c p) d -> p (l c) d", p=P)).then_inc(s["wo_in"], 16)
                    sp.wait_ge(s["out_full"], 1 + B * L + 1)
                    sp.dma_start(w1[:, :], a["W1"][ds(L, 1), :, :].rearrange("l p n -> p (l n)")).then_inc(s["w12_in"], 16)
                    for c, (h0, m) in enumerate(HCH):
                        sp.dma_start(w2[0:m, c, :], a["W2"][ds(L, 1), h0:h0 + m, :].rearrange("l p n -> p (l n)")).then_inc(s["w12_in"], 16)
                sp.wait_ge(s["w12_in"], 1 + 16 * 4 * LAYERS)

            @block.tensor
            def _(pe):
                def turn_bank(kk, j, i, L):
                    u = turn_units(kk) + i
                    pe.wait_ge(s["t_evac"], 1 + TURN_LAYER * L + u + 1)
                    return 2 + (turn_units(j if isinstance(kk, int) and kk < 4 else (4 + j) if not isinstance(kk, int) else kk) + i) % 2

                def unit(L, kk, i, fill):
                    u = 8 * (LT * L + kk) + i
                    pe.wait_ge(s["proj_evac"], 1 + u + 1)
                    fill(psum[:, i % 2, :]).then_inc(s["proj_full"], 1)

                def project_v(bank, p, w):
                    for par in range(2):
                        heads = wqkv[:, 2 * INNER:].rearrange("p (c r e) -> p r c e", r=2, e=DH)[:, par, :, :]
                        last = pe.matmul(bank[DH * par:DH * (par + 1), :], xs[:, p, WIN * w:WIN * w + 2 * WIN], heads,
                                         start=True, stop=True)
                    return last

                def step(L, b, j, kk):
                    i = 0
                    if on(kk, 0):
                        p = j % 2
                        if isinstance(kk, int) and kk == 0:
                            pe.wait_ge(s["wqkv_in"], 1 + 16 * L + 16)
                        pe.wait_ge(s["xs_ready"], 1 + 2 * (LT * L + kk) + 2)
                        for n in range(4):
                            unit(L, kk, n, lambda bank: pe.matmul(bank, xs[:, p, WIN:WIN + P], wqkv[:, 512 * n:512 * (n + 1)],
                                                                  start=True, stop=True))
                    if on(kk, 3):
                        if isinstance(kk, int) and kk == 3:
                            pe.wait_ge(s["wo_in"], 1 + 16 * L + 16)
                        u_ot = turn_units(kk)
                        bank = turn_bank(kk, j, i, L)
                        pe.wait_ge(s["t_evac"], 1 + TURN_LAYER * L + u_ot + 2)
                        for c in range(PAIRS):
                            last = pe.matmul(psum[:, bank, 0:P], wo[:, c, :], oT[:, c, :], start=(c == 0), stop=(c == PAIRS - 1))
                        last.then_inc(s["wo_done"], 1)
                        i += 1
                    if on(kk, 2):
                        pe.wait_ge(s["exp_done"], 1 + LT * L + kk - 2 + 1)
                        for n in range(2):
                            bank = turn_bank(kk, j, i, L)
                            for c in range(4):
                                last = pe.transpose(psum[:, bank, c * P:(c + 1) * P],
                                                    prob[:, 8 * n + 2 * c:8 * n + 2 * c + 2, :].rearrange("p h w -> p (h w)"), k.ident[:, :])
                            last.then_inc(s["t_full"], 1)
                            i += 1
                        pt_end = i
                    if on(kk, 1):
                        pe.wait_ge(s["add_done"], 1 + 2 * (LT * L + kk - 1) + 2 + 2)
                        for n in range(4):
                            bank = turn_bank(kk, j, i, L)
                            for c in range(4):
                                h = 8 * (n % 2) + 2 * c
                                last = pe.transpose(psum[:, bank, c * P:(c + 1) * P],
                                                    rope[:, (j - 1) % 2, n // 2, h:h + 2, :].rearrange("p h e -> p (h e)"), k.ident[:, :])
                            last.then_inc(s["t_full"], 1)
                            i += 1
                        tqk_end = i
                    if on(kk, 2):
                        g = LT * L + kk - 2
                        pe.wait_ge(s["t_evac"], 1 + TURN_LAYER * L + turn_units(kk) + pt_end + 2)
                        pe.wait_ge(s["proj_evac"], 1 + 8 * g + 8 + 2)
                        pe.wait_ge(s["on_done"], 1 + g + 1)
                        for w in range(WPT):
                            for c in range(PAIRS):
                                last = pe.matmul(psum[WIN * w:WIN * (w + 1), 6 + c // 4, (c % 4) * P:(c % 4 + 1) * P],
                                                 probT[:, c, WIN * w:WIN * (w + 1)],
                                                 v2[:, (j - 2) % 2, w, c, :, :].rearrange("p r e -> p (r e)"), start=True, stop=True)
                        last.then_inc(s["pv_done"], 1)
                    if on(kk, 1):
                        g = LT * L + kk - 1
                        sj = (j - 1) % 4
                        pe.wait_ge(s["t_evac"], 1 + TURN_LAYER * L + turn_units(kk) + tqk_end + 2)
                        pe.wait_ge(s["sub_done"], 1 + g + 1)
                        for half in range(2):
                            pe.matmul(psum[:, 4 + half, :], k.ident_bf[:, :], k.band[:, int(sj == 0), :, :].rearrange("p h w -> p (h w)"),
                                      start=True, stop=False, skip_group_check=True)
                        for w in range(WPT):
                            t0 = P * (sj % 2) + WIN * w
                            for c in range(PAIRS):
                                last = pe.matmul(psum[WIN * w:WIN * (w + 1), 4 + c // 4, (c % 4) * P:(c % 4 + 1) * P],
                                                 qT[:, c, WIN * w:WIN * (w + 1)], kT[:, c, :, t0:t0 + 2 * WIN],
                                                 start=False, stop=True, skip_group_check=True)
                        last.then_inc(s["scores"], 1)
                    if on(kk, 0):
                        for w in range(WPT):
                            unit(L, kk, 4 + w, lambda bank: project_v(bank, p, w))
                    if on(kk, 2):
                        pe.wait_ge(s["on_done"], 1 + LT * L + kk - 2 + 2)
                        for n in range(2):
                            bank = turn_bank(kk, j, i, L)
                            for c in range(4):
                                h = 8 * n + 2 * c
                                last = pe.transpose(psum[:, bank, c * P:(c + 1) * P],
                                                    o_tok[:, h:h + 2, :].rearrange("p h e -> p (h e)"), k.ident[:, :])
                            last.then_inc(s["t_full"], 1)
                            i += 1

                def feed_forward(L):
                    ln_tensor(pe, k, s, lambda b: xn[:, b, :], B * L, lambda b: pe.wait_ge(s["shifted"], 1 + 2 * (B * L + b) + 2))
                    pe.wait_ge(s["w12_in"], 1 + 64 * L + 64)
                    for b in range(B):
                        pe.wait_ge(s["ln_done"], 1 + B * L + b + 1)
                        for c, (h0, m) in enumerate(HCH):
                            for which in range(2):
                                n = 3 * b + c
                                full, evac = (s["gate_full"], s["gate_evac"]) if which == 0 else (s["val_full"], s["val_evac"])
                                if n >= 2:
                                    pe.wait_ge(evac, 1 + 12 * L + n - 1)
                                col = (HID if which == 0 else 0) + h0
                                pe.matmul(psum[0:m, 4 + 2 * which + n % 2, :], w1[:, col:col + m], xn[:, b, :],
                                          start=True, stop=True).then_inc(full, 1)
                        pe.wait_ge(s["val_evac"], 1 + 12 * L + 3 * b + 3)
                        if b >= 2:
                            pe.wait_ge(s["out_evac"], 1 + B * L + b - 1)
                        for c, (h0, m) in enumerate(HCH):
                            last = pe.matmul(psum[:, b % 2, :], w2[0:m, c, :], hid[0:m, b % 2, c, :], start=(c == 0), stop=(c == 2))
                        last.then_inc(s["out_full"], 1)

                with pe.Fori(0, LAYERS) as L:
                    steps(pe, step, L)
                    feed_forward(L)

            @block.scalar
            def _(act):
                act.sem_inc(s["proj_evac"], 2)
                act.sem_inc(s["t_evac"], 2)

                def step(L, b, j, kk):
                    u_t = TURN_LAYER * L + turn_units(kk)
                    i = 0

                    def evac(out, bank, source=None):
                        return act.activation(out, psum[:, bank, :] if source is None else source, ACT.Copy)

                    def t_bank(i):
                        static = turn_units(4 + j) if not isinstance(kk, int) else turn_units(kk)
                        return 2 + (static + i) % 2

                    g0 = LT * L + kk
                    if on(kk, 0):
                        for n in range(4):
                            act.wait_ge(s["proj_full"], 1 + 8 * g0 + n + 1)
                            if n % 2 == 0:
                                act.wait_ge(s["rot_done"], 1 + 2 * g0 + n // 2 + 1)
                            evac(raw[:, n // 2, 8 * (n % 2):8 * (n % 2) + 8, :].rearrange("p h e -> p (h e)"), n % 2).then_inc(s["proj_evac"], 1)
                        for half in range(2):
                            act.wait_ge(s["proj_evac"], 1 + 8 * g0 + 2 * half + 2 + 2)
                            act.wait_ge(s["ss_done"], 1 + 2 * g0 + half + 1)
                            act.activation(sq[:, half, :, :], raw[:, half, :, :], ACT.Square).then_inc(s["sq_done"], 1)
                    if on(kk, 3):
                        act.wait_ge(s["wo_done"], 1 + g0 - 3 + 2)
                        act.wait_ge(s["res_done"], 1 + g0 - 3 + 1)
                        evac(wo_sb[:, :], 0, psum[:, t_bank(i), 0:P]).then_inc(s["t_evac"], 1)
                        i += 1
                    if on(kk, 2):
                        act.wait_ge(s["pv_done"], 1 + g0 - 2)
                        for n in range(2):
                            act.wait_ge(s["t_full"], 1 + u_t_full(L, kk, i))
                            evac(probT[:, 4 * n:4 * n + 4, :].rearrange("p c t -> p (c t)"), t_bank(i)).then_inc(s["t_evac"], 1)
                            i += 1
                    if on(kk, 1):
                        sj = (j - 1) % 4
                        slot = WIN + P * (sj % 2)
                        act.wait_ge(s["scores"], 1 + g0 - 1)
                        for n in range(2):
                            act.wait_ge(s["t_full"], 1 + u_t_full(L, kk, i))
                            evac(qT[:, 4 * n:4 * n + 4, :].rearrange("p c t -> p (c t)"), t_bank(i)).then_inc(s["t_evac"], 1)
                            i += 1
                        for n in range(2):
                            act.wait_ge(s["t_full"], 1 + u_t_full(L, kk, i))
                            turned = psum[:, t_bank(i), :].rearrange("p (c t) -> p c t", c=4)
                            for par in range(2):
                                rows = slice(DH * par, DH * (par + 1))
                                if sj == 1:
                                    evac(kT[rows, 4 * n:4 * n + 4, par, 0:WIN], 0, turned[rows, :, P - WIN:P])
                                last = evac(kT[rows, 4 * n:4 * n + 4, par, slot:slot + P], 0, turned[rows, :, :])
                            last.then_inc(s["t_evac"], 1)
                            i += 1
                    if on(kk, 0):
                        act.wait_ge(s["pv_done"], 1 + g0 - 1) if not isinstance(kk, int) or kk >= 2 else act.wait_ge(s["pv_done"], 1 + LT * L)
                        for w in range(WPT):
                            act.wait_ge(s["proj_full"], 1 + 8 * g0 + 4 + w + 1)
                            for par in range(2):
                                rows = slice(DH * par, DH * (par + 1))
                                last = evac(v2[rows, j % 2, w, :, par, :], 0, psum[rows, w % 2, :].rearrange("p (c e) -> p c e", e=DH))
                            last.then_inc(s["proj_evac"], 1)
                    if on(kk, 1):
                        act.wait_ge(s["sub_done"], 1 + g0 - 1 + 2)
                        act.activation(prob[:, :, :], prob[:, :, :], ACT.Exp).then_inc(s["exp_done"], 1)
                    if on(kk, 2):
                        act.wait_ge(s["wo_done"], 1 + g0 - 2 + 1)
                        for n in range(2):
                            act.wait_ge(s["t_full"], 1 + u_t_full(L, kk, i))
                            evac(oT[:, 4 * n:4 * n + 4, :].rearrange("p c t -> p (c t)"), t_bank(i)).then_inc(s["t_evac"], 1)
                            i += 1

                def u_t_full(L, kk, i):
                    before = turn_units(kk) - min(max(kk - 2, 0), LT) if isinstance(kk, int) else 8 * kk - 13
                    return 8 * LT * L + before + i + 1

                with act.Fori(0, LAYERS) as L:
                    steps(act, step, L)
                    ln_scalar(act, k, s, lambda b: xn[:, b, :], B * L)
                    for b in range(B):
                        for c, (h0, m) in enumerate(HCH):
                            n = 3 * b + c
                            if n >= 2:
                                act.wait_ge(s["val_evac"], 1 + 12 * L + n - 1)
                            wait_alone(act, s["gate_full"], 12 * L + n + 1, s["scrap"])
                            act.activation(gate[0:m, n % 2, :], psum[0:m, 4 + n % 2, :], ACT.Gelu,
                                           bias=k.b1[0:m, ds(L, 1), 1, c]).then_inc(s["gate_evac"], 1)

            @block.vector
            def _(dve):
                dve.memset(kT[:, :, :, :], 0.0).then_inc(s["zeroed"], 1)
                dve.memset(v2[:, :, :, :, :, :], 0.0).then_inc(s["zeroed"], 1)
                dve.wait_ge(s["zeroed"], 1 + 2)
                for sem, n in ((s["rot_done"], 2), (s["ss_done"], 2), (s["sub_done"], 1), (s["on_done"], 1)):
                    dve.sem_inc(sem, n)

                def newton(g):
                    at = [0]

                    def link(ins):
                        at[0] += 1
                        ins.then_inc(s["newton"], 1)
                        wait_alone(dve, s["newton"], NEWTON * g + at[0], s["scrap"]) if at[0] == 2 else dve.wait_ge(s["newton"], 1 + NEWTON * g + at[0])

                    x, h, y, z = (nt[:, n, :] for n in range(4))
                    link(dve.tensor_scalar(x, ss[:, :], 1e-24, None, ALU.max))
                    link(dve.tensor_scalar(h.bitcast(U32), x.bitcast(U32), 1, 0xFFFFFFFF, ALU.logical_shift_right, ALU.bitwise_xor))
                    link(dve.tensor_tensor(y.bitcast(U32), h.bitcast(U32), k.magic[:, :], ALU.add))
                    for n in range(3):
                        link(dve.scalar_tensor_tensor(z, y, -0.5, y, ALU.mult, ALU.mult))
                        link(dve.tensor_tensor(h, z, x, ALU.mult))
                        if n == 2:
                            dve.wait_ge(s["norm_done"], 1 + 2 * g)
                            dve.scalar_tensor_tensor(rn[:, :], h, 1.5, y, ALU.add, ALU.mult).then_inc(s["rn_ready"], 1)
                        else:
                            link(dve.scalar_tensor_tensor(y, h, 1.5, y, ALU.add, ALU.mult))

                def shifted(L, b, j, t):
                    late = not isinstance(t, int) or t >= 2
                    dve.wait_ge(s["proj_evac"], 1 + 8 * (LT * L + (t - 1 if late else 0)) + 2)
                    t0 = PAD - WIN + P * j
                    dve.tensor_copy(xs[0:DH, j % 2, :], tile(k.XA, 0, DH, b, t0)).then_inc(s["xs_ready"], 1)
                    dve.tensor_copy(xs[DH:P, j % 2, :], tile(k.XA, DH, P, b, t0 - 1)).then_inc(s["xs_ready"], 1)

                def rotate(g, j, half):
                    hd = DH // 2
                    dve.wait_ge(s["norm_done"], 1 + 2 * g + half + 1)
                    cos = rot[:, half, j, :].unsqueeze(1).to_broadcast([P, H, DH])
                    dve.tensor_tensor(rope[:, j % 2, half, :, :], raw[:, half, :, :], cos, ALU.mult)
                    dve.wait_ge(s["add_done"], 1 + 2 * g + half + 1)
                    for q in range(2):
                        sin = rot[:, 2 + half, j, hd * q:hd * (q + 1)].unsqueeze(1).to_broadcast([P, H, hd])
                        last = dve.tensor_tensor(t2[:, half, :, hd * q:hd * (q + 1)], raw[:, half, :, hd * (1 - q):hd * (2 - q)], sin, ALU.mult)
                    last.then_inc(s["rot_done"], 1)

                def step(L, b, j, kk):
                    g0 = LT * L + kk
                    if on(kk, 0):
                        if isinstance(kk, int) and kk == 0:
                            dve.wait_ge(s["out_evac"], 1 + B * L)
                        if j == 0:
                            shifted(L, b, 0, kk)
                        if j < 3:
                            shifted(L, b, j + 1, kk + 1)
                        for half in range(2):
                            dve.wait_ge(s["sq_done"], 1 + 2 * g0 + half + 1)
                            dve.tensor_reduce(ss[:, H * half:H * (half + 1)], sq[:, half, :, :], AX_X, ALU.add).then_inc(s["ss_done"], 1)
                        dve.wait_ge(s["ss_done"], 1 + 2 * g0 + 2 + 2)
                        newton(g0)
                    if on(kk, 2):
                        g = g0 - 2
                        dve.wait_ge(s["pv_done"], 1 + g + 1)
                        dve.wait_ge(s["rden_done"], 1 + g + 1)
                        dve.wait_ge(s["wo_done"], 1 + g + 1)
                        dve.tensor_tensor(o_tok[:, :, :], psum[:, 6:8, :].rearrange("p a n -> p (a n)").rearrange("p (h e) -> p h e", e=DH),
                                          rden[:, (j - 2) % 2, :].unsqueeze(2).to_broadcast([P, H, DH]), ALU.mult).then_inc(s["on_done"], 1)
                    if on(kk, 0):
                        if not isinstance(kk, int) or kk >= 2:
                            dve.wait_ge(s["scores"], 1 + g0 - 1)
                        rotate(g0, j, 0)
                    if on(kk, 1):
                        g = g0 - 1
                        sc = psum[:, 4:6, :].rearrange("p a n -> p (a n)").rearrange("p (h w) -> p h w", w=2 * WIN)
                        dve.wait_ge(s["scores"], 1 + g + 1)
                        dve.tensor_reduce(top[:, :], sc, AX_X, ALU.max).then_inc(s["top"], 1)
                        dve.wait_ge(s["top"], 1 + g + 1)
                        dve.wait_ge(s["pv_done"], 1 + g)
                        dve.tensor_tensor(prob[:, :, :], sc, top[:, :].unsqueeze(2).to_broadcast([P, H, 2 * WIN]),
                                          ALU.subtract).then_inc(s["sub_done"], 1)
                    if on(kk, 0):
                        rotate(g0, j, 1)
                    if on(kk, 1):
                        g = g0 - 1
                        dve.wait_ge(s["exp_done"], 1 + g + 1)
                        dve.tensor_reduce(den[:, :], prob[:, :, :], AX_X, ALU.add).then_inc(s["summed"], 1)
                        dve.wait_ge(s["summed"], 1 + g + 1)
                        dve.reciprocal(rden[:, (j - 1) % 2, :], den[:, :]).then_inc(s["rden_done"], 1)

                with dve.Fori(0, LAYERS) as L:
                    hd = DH // 2
                    for half in range(2):
                        gain = k.qk_gain[:, half, ds(L, 1), :]
                        dve.tensor_tensor(rot[:, half, :, :], k.rot_base[:, half, :, :], gain.to_broadcast([P, TILES, DH]), ALU.mult)
                        for q in range(2):
                            dve.tensor_tensor(rot[:, 2 + half, :, hd * q:hd * (q + 1)], k.rot_base[:, 2 + half, :, hd * q:hd * (q + 1)],
                                              k.qk_gain[:, half, ds(L, 1), hd * (1 - q):hd * (2 - q)].to_broadcast([P, TILES, hd]),
                                              ALU.mult).then_inc(s["tabled"], 1)
                    dve.wait_ge(s["tabled"], 1 + 4 * L + 4)
                    steps(dve, step, L)
                    for b in range(B):
                        dve.wait_ge(s["res_done"], 1 + LT * L + TILES * (b + 1) + 1)
                        dve.tensor_copy(xn[0:DH, b, :], k.XB[0:DH, b, PAD:ROW]).then_inc(s["shifted"], 1)
                        dve.tensor_copy(xn[DH:P, b, :], k.XB[DH:P, b, PAD - 1:ROW - 1]).then_inc(s["shifted"], 1)
                    ln_vector(dve, k, s, lambda b: xn[:, b, :], lambda b: xn[:, b, :], B * L,
                              k.ln_g[:, ds(L, 1)], k.ln_b[:, ds(L, 1)])
                    for b in range(B):
                        for c, (h0, m) in enumerate(HCH):
                            n = 3 * b + c
                            dve.wait_ge(s["val_full"], 1 + 12 * L + n + 1)
                            dve.wait_ge(s["gate_evac"], 1 + 12 * L + n + 1)
                            if b >= 2 and c == 0:
                                dve.wait_ge(s["out_full"], 1 + B * L + b)
                            dve.scalar_tensor_tensor(hid[0:m, b % 2, c, :], psum[0:m, 6 + n % 2, :], k.b1[0:m, ds(L, 1), 0, c],
                                                     gate[0:m, n % 2, :], ALU.add, ALU.mult).then_inc(s["val_evac"], 1)
                        dve.wait_ge(s["out_full"], 1 + B * L + b + 1 + 1)
                        dve.scalar_tensor_tensor(k.XA[:, b, PAD:ROW], psum[:, b % 2, :], k.b2[:, ds(L, 1)], k.XB[:, b, PAD:ROW],
                                                 ALU.add, ALU.add).then_inc(s["out_evac"], 1)

            @block.gpsimd
            def _(pool):
                pool.sem_inc(s["wo_done"], 1)
                pool.sem_inc(s["out_full"], 1)
                pool.sem_inc(s["add_done"], 2)
                pool.sem_inc(s["res_done"], 1)

                def step(L, b, j, kk):
                    g0 = LT * L + kk
                    if on(kk, 0):
                        for half in range(2):
                            pool.wait_ge(s["rn_ready"], 1 + g0 + 1)
                            pool.tensor_tensor(raw[:, half, :, :], raw[:, half, :, :],
                                               rn[:, H * half:H * (half + 1)].unsqueeze(2).to_broadcast([P, H, DH]), ALU.mult).then_inc(s["norm_done"], 1)
                    if on(kk, 3):
                        pool.wait_ge(s["t_evac"], 1 + TURN_LAYER * L + turn_units(kk) + 1 + 2)
                        jj, bb = (j - 3) % 4, (b if j == 3 else b - 1)
                        t0 = PAD + P * jj
                        pool.tensor_tensor(tile(k.XB, 0, P, bb, t0, P), wo_sb[:, :], tile(k.XA, 0, P, bb, t0, P), ALU.add).then_inc(s["res_done"], 1)
                    if on(kk, 0):
                        for half in range(2):
                            pool.wait_ge(s["rot_done"], 1 + 2 * g0 + half + 1 + 2)
                            pool.tensor_tensor(rope[:, j % 2, half, :, :], rope[:, j % 2, half, :, :], t2[:, half, :, :], ALU.add).then_inc(s["add_done"], 1)

                with pool.Fori(0, LAYERS) as L:
                    steps(pool, step, L)




def mamba_phase(k, a):
    nc = k.nc
    psum = k.psum
    with ExitStack() as ctx:
        load = names(ctx, "mw", nc, "loaded", "turned", "copied", "done")
        s = names(ctx, "mb", nc, "zeroed", "xz_full", "xz_evac", "conv_in", "conv_step", "silu", "u_done", "xd_full", "xd_evac", "dt_full", "dt_in", "dt_abs",
                  "dt_exp", "dt_ln", "dt_max", "dt_done", "sel", "bc_full", "b_used", "c_copied", "da_done", "dbu", "scanned", "hc_done",
                  "y_full", "y_evac", "y_step", "yg_done", "out_full", "out_done", "staged", "copied", "scrap")

        def sb(name, shape, dt=F32):
            return ctx.enter_context(nc.sbuf_tensor(f"mb_{name}", shape, dt))

        w_inT = sb("w_inT", [P, 2 * DI])
        w_xT = sb("w_xT", [P, CI, XD])
        w_dtT = sb("w_dtT", [DR, DI])
        w_outT = sb("w_outT", [P, CI, D])
        conv_w = sb("conv_w", [P, CI, DC])
        conv_b = sb("conv_b", [P, CI])
        b_dt = sb("b_dt", [P, CI])
        skip = sb("skip", [P, CI])
        neg_a = sb("neg_a", [P, CI, DS])
        sel = sb("sel", [P, 2 * DS, P])
        w_nat = sb("w_nat", [P, 4, P])
        wx_nat = sb("wx_nat", [XD, DI])
        wdt_nat = sb("wdt_nat", [P, CI, DR])
        wo_nat = sb("wo_nat", [P, DI])
        vec_nat = sb("vec_nat", [CI, 3, P])
        xp = sb("xp", [P, CI, DC - 1 + N])
        zb = sb("zb", [P, CI, B, N])
        u = sb("u", [P, CI, B, N])
        dt = sb("dt", [P, CI, B, N])
        xd = sb("xd", [P, B, N])
        conv = sb("conv", [P, CI, N])
        dtr = sb("dtr", [DR, N])
        tmp = sb("tmp", [P, CI, N])
        dtu = sb("dtu", [P, CI, N])
        c_sb = sb("c_sb", [P, 2, N])
        da = sb("da", [P, 4, N])
        dbu = sb("dbu", [P, 4, N])
        hs = sb("hs", [P, 4, N])
        hc = sb("hc", [P, 4, N])
        yg = sb("yg", [P, CI, N])

        with nc.Block() as block:
            @block.sync
            def _(sp):
                sp.dma_start(w_nat[:, :, :], a["W_in"].rearrange("(c p) d -> p c d", p=P)).then_inc(load["loaded"], 16)
                sp.dma_start(wx_nat[:, :], a["W_x"]).then_inc(load["loaded"], 16)
                sp.dma_start(wdt_nat[:, :, :], a["W_dt"].rearrange("(c p) r -> p c r", p=P)).then_inc(load["loaded"], 16)
                sp.dma_start(wo_nat[:, :], a["W_out"]).then_inc(load["loaded"], 16)
                sp.dma_start(conv_w[:, :, :], a["conv_w"].rearrange("(c p) o t -> p c (o t)", p=P)).then_inc(load["loaded"], 16)
                sp.dma_start(neg_a[:, :, :], a["A_log"].rearrange("(c p) n -> p c n", p=P)).then_inc(load["loaded"], 16)
                for i, v in enumerate((a["conv_b"], a["b_dt"], a["D"])):
                    sp.dma_start(vec_nat[:, i, :], v.rearrange("(c p) -> c p", p=P)).then_inc(load["loaded"], 16)

            @block.tensor
            def _(pe):
                pe.wait_ge(load["loaded"], 1 + 16 * 9)
                for c in range(4):
                    last = pe.transpose(psum[:, 0, c * P:(c + 1) * P], w_nat[:, c, :], k.ident[:, :])
                last.then_inc(load["turned"], 1)
                for c in range(CI):
                    pe.transpose(psum[:, 1, c * XD:(c + 1) * XD], wx_nat[:, c * P:(c + 1) * P], k.ident[0:XD, 0:XD])
                    pe.transpose(psum[0:DR, 2, c * P:(c + 1) * P], wdt_nat[:, c, :], k.ident[:, :])
                    last = pe.transpose(psum[:, 3, c * P:(c + 1) * P], wo_nat[:, c * P:(c + 1) * P], k.ident[:, :])
                for i in range(3):
                    last = pe.transpose(psum[:, 4, CI * i:CI * (i + 1)], vec_nat[:, i, :], k.ident[0:CI, 0:CI])
                last.then_inc(load["turned"], 1)

            @block.vector
            def _(dve):
                dve.wait_ge(load["turned"], 1 + 2)
                for i, t in enumerate((conv_b, b_dt, skip)):
                    dve.tensor_copy(t[:, :], psum[:, 4, CI * i:CI * (i + 1)])
                dve.tensor_copy(w_inT[:, :], psum[:, 0, :])
                dve.tensor_copy(w_xT[:, :, :], psum[:, 1, 0:CI * XD].rearrange("p (c x) -> p c x", c=CI))
                dve.tensor_copy(w_dtT[:, :], psum[0:DR, 2, 0:DI])
                dve.tensor_copy(w_outT[:, :, :], psum[:, 3, 0:DI].rearrange("p (c d) -> p c d", c=CI))
                dve.wait_ge(load["loaded"], 1 + 16 * 9)
                dve.tensor_scalar(neg_a[:, :, :], neg_a[:, :, :], 80.0, None, ALU.min).then_inc(load["copied"], 1)
                dve.wait_ge(load["done"], 1 + 1)
                dve.tensor_scalar(neg_a[:, :, :], neg_a[:, :, :], -1.0, None, ALU.mult)

            @block.scalar
            def _(act):
                act.wait_ge(load["copied"], 1 + 1)
                act.activation(neg_a[:, :, :], neg_a[:, :, :], ACT.Exp).then_inc(load["done"], 1)

            @block.gpsimd
            def _(pool):
                pool.memset(xd[:, :, :], 0.0)
                pool.memset(xp[:, :, :], 0.0)
                pool.memset(sel[:, :, :], 0.0).then_inc(s["zeroed"], 1)
                pool.wait_ge(s["zeroed"], 1 + 1)
                pool.affine_select(out=sel[:, :, :], in_=sel[:, :, :], compare_op=ALU.not_equal, fill=1.0, base=-DR,
                                   pattern=[[-1, 2 * DS], [0, P]], channel_multiplier=1).then_inc(s["sel"], 1)

        with nc.Block() as block:
            @block.tensor
            def _(pe):
                with pe.Fori(0, B) as b:
                    pe.wait_ge(s["xz_evac"], 1 + 4 * b) 
                    for c in range(4):
                        pe.matmul(psum[:, c, :], w_inT[:, c * P:(c + 1) * P], tokens(k.XA, b), start=True, stop=True).then_inc(s["xz_full"], 1)
                    pe.wait_ge(s["u_done"], 1 + CI * b + CI)
                    for c in range(CI):
                        last = pe.matmul(psum[0:XD, 4, :], w_xT[:, c, :], batch(u, c, b), start=(c == 0), stop=(c == CI - 1))
                    last.then_inc(s["xd_full"], 1)
                    pe.wait_ge(s["xd_evac"], 1 + b + 1)
                    for c in range(CI):
                        pe.matmul(psum[:, 5 + c, :], w_dtT[:, c * P:(c + 1) * P], dtr[:, :], start=True, stop=True).then_inc(s["dt_full"], 1)

            @block.vector
            def _(dve):
                with dve.Fori(0, B) as b:
                    for c in range(CI):
                        dve.wait_ge(s["xz_full"], 1 + 4 * b + c + 1)
                        dve.tensor_scalar(xp[:, c, DC - 1:DC - 1 + N], psum[:, c, :], 0.0, 1.0, ALU.max, ALU.min).then_inc(s["xz_evac"], 1)
                    for c in range(CI):
                        dve.wait_ge(s["xz_full"], 1 + 4 * b + CI + c + 1)
                        dve.tensor_scalar(batch(zb, c, b), psum[:, CI + c, :], 0.0, 1.0, ALU.max, ALU.min).then_inc(s["xz_evac"], 1)
                    for c in range(CI):
                        dve.wait_ge(s["xz_evac"], 1 + 4 * b + c + 1)
                        dve.tensor_scalar(conv[:, c, :], xp[:, c, 0:N], conv_w[:, c, 0:1], None, ALU.mult).then_inc(s["conv_step"], 1)
                        for t in range(1, DC):
                            dve.wait_ge(s["conv_step"], 1 + DC * (CI * b + c) + t)
                            dve.scalar_tensor_tensor(conv[:, c, :], xp[:, c, t:t + N], conv_w[:, c, t:t + 1], conv[:, c, :],
                                                     ALU.mult, ALU.add).then_inc(s["conv_step"], 1)
                    for c in range(CI):
                        dve.wait_ge(s["silu"], 1 + CI * b + c + 1)
                        dve.tensor_scalar(batch(u, c, b), conv[:, c, :], 0.0, 1.0, ALU.max, ALU.min).then_inc(s["u_done"], 1)
                    dve.wait_ge(s["xd_full"], 1 + b + 1)
                    dve.tensor_scalar(dtr[:, :], psum[0:DR, 4, :], 0.0, 1.0, ALU.max, ALU.min).then_inc(s["xd_evac"], 1)
                    for c in range(CI):
                        dve.wait_ge(s["dt_full"], 1 + CI * b + c + 1)
                        dve.tensor_scalar(conv[:, c, :], psum[:, 5 + c, :], b_dt[:, c:c + 1], None, ALU.add).then_inc(s["dt_in"], 1)
                        dve.wait_ge(s["dt_in"], 1 + CI * b + c + 1)
                        dve.scalar_tensor_tensor(tmp[:, c, :], conv[:, c, :], -1.0, conv[:, c, :], ALU.mult, ALU.min).then_inc(s["dt_abs"], 1)
                        dve.tensor_scalar(batch(dt, c, b), conv[:, c, :], 0.0, None, ALU.max).then_inc(s["dt_max"], 1)
                    for c in range(CI):
                        dve.wait_ge(s["dt_ln"], 1 + CI * b + c + 1)
                        dve.wait_ge(s["dt_max"], 1 + CI * b + c + 1)
                        dve.tensor_tensor(batch(dt, c, b), batch(dt, c, b), tmp[:, c, :], ALU.add).then_inc(s["dt_done"], 1)
                        dve.wait_ge(s["dt_done"], 1 + 2 * (CI * b + c) + 1)
                        dve.tensor_scalar(batch(dt, c, b), batch(dt, c, b), 1e-4, 20.0, ALU.max, ALU.min).then_inc(s["dt_done"], 1)

            @block.scalar
            def _(act):
                with act.Fori(0, B) as b:
                    for c in range(CI):
                        act.wait_ge(s["conv_step"], 1 + DC * (CI * b + c + 1))
                        act.activation(conv[:, c, :], conv[:, c, :], ACT.Silu, bias=conv_b[:, c:c + 1]).then_inc(s["silu"], 1)
                    wait_alone(act, s["xd_evac"], b + 1, s["scrap"])
                    act.activation(batch3(xd, b), psum[0:XD, 4, :], ACT.Copy).then_inc(s["copied"], 1)
                    for c in range(CI):
                        act.wait_ge(s["dt_abs"], 1 + CI * b + c + 1)
                        act.activation(tmp[:, c, :], tmp[:, c, :], ACT.Exp).then_inc(s["dt_exp"], 1)
                    for c in range(CI):
                        act.wait_ge(s["dt_exp"], 1 + CI * b + c + 1)
                        act.activation(tmp[:, c, :], tmp[:, c, :], ACT.Ln, bias=k.one[:, 0:1]).then_inc(s["dt_ln"], 1)
                for c in range(CI):
                    act.wait_ge(s["xz_evac"], 1 + 4 * B)
                    act.activation(zb[:, c, :, :], zb[:, c, :, :], ACT.Silu)

        with nc.Block() as block:
            @block.tensor
            def _(pe):
                with pe.Fori(0, B) as b:
                    def sums(n):
                        for c in range(CI):
                            pe.wait_ge(s["hc_done"], 1 + CI * DS * b + CI * n + c + 1)
                            if n == 0 and c == 0:
                                pe.wait_ge(s["y_evac"], 1 + CI * b)
                            pe.matmul(psum[:, 4 + c, :], k.ident[:, :], hc[:, (CI * n + c) % 4, :], start=(n == 0), stop=(n == DS - 1),
                                      skip_group_check=True).then_inc(s["y_full"], 1)

                    for n in range(DS):
                        if n >= 2:
                            pe.wait_ge(s["b_used"], 1 + CI * (DS * b + n - 1))
                            pe.wait_ge(s["c_copied"], 1 + DS * b + n - 1)
                        else:
                            pe.wait_ge(s["b_used"], 1 + CI * DS * b)
                            pe.wait_ge(s["c_copied"], 1 + DS * b)
                        for which in range(2):
                            pe.matmul(psum[:, 2 * which + n % 2, :], sel[:, DS * which + n, :], batch3(xd, b, P), start=True, stop=True).then_inc(s["bc_full"], 1)
                        if n >= 2:
                            sums(n - 2)
                    sums(DS - 2)
                    sums(DS - 1)
                    pe.wait_ge(s["yg_done"], 1 + CI * b + CI)
                    for c in range(CI):
                        last = pe.matmul(psum[:, 6, :], w_outT[:, c, :], yg[:, c, :], start=(c == 0), stop=(c == CI - 1))
                    last.then_inc(s["out_full"], 1)

            @block.scalar
            def _(act):
                with act.Fori(0, B) as b:
                    for n in range(DS):
                        m0 = CI * (DS * b + n)
                        for c in range(CI):
                            wait_alone(act, s["scanned"], m0 + c - 3 if CI * n + c >= 4 else CI * DS * b, s["scrap"])
                            act.activation(da[:, (CI * n + c) % 4, :], batch(dt, c, b), ACT.Exp, scale=neg_a[:, c, n:n + 1]).then_inc(s["da_done"], 1)
                        act.wait_ge(s["bc_full"], 1 + 2 * (DS * b + n) + 2)
                        if n >= 2:
                            act.wait_ge(s["hc_done"], 1 + m0 - 2)
                        else:
                            act.wait_ge(s["hc_done"], 1 + CI * DS * b)
                        act.activation(c_sb[:, n % 2, :], psum[:, 2 + n % 2, :], ACT.Copy).then_inc(s["c_copied"], 1)

            @block.vector
            def _(dve):
                with dve.Fori(0, B) as b:
                    for c in range(CI):
                        dve.tensor_tensor(dtu[:, c, :], batch(dt, c, b), batch(u, c, b), ALU.mult).then_inc(s["staged"], 1)
                    dve.wait_ge(s["staged"], 1 + CI * b + CI)
                    for n in range(DS):
                        for c in range(CI):
                            i = CI * n + c
                            m = CI * DS * b + i
                            dve.wait_ge(s["bc_full"], 1 + 2 * (DS * b + n) + 1)
                            dve.tensor_tensor(dbu[:, i % 4, :], dtu[:, c, :], psum[:, n % 2, :], ALU.mult).then_inc(s["b_used"], 1)
                            dve.wait_ge(s["b_used"], 1 + m + 1)
                            dve.wait_ge(s["da_done"], 1 + m + 1)
                            if i >= 4:
                                dve.wait_ge(s["hc_done"], 1 + m - 3)
                            dve.tensor_tensor_scan(hs[:, i % 4, :], da[:, i % 4, :], dbu[:, i % 4, :], 0.0, ALU.mult, ALU.add).then_inc(s["scanned"], 1)
                    for c in range(CI):
                        dve.wait_ge(s["y_full"], 1 + CI * DS * b + CI * (DS - 1) + c + 1)
                        dve.scalar_tensor_tensor(tmp[:, c, :], batch(u, c, b), skip[:, c:c + 1], psum[:, 4 + c, :], ALU.mult, ALU.add).then_inc(s["y_evac"], 1)
                        dve.wait_ge(s["y_evac"], 1 + CI * b + c + 1)
                        dve.tensor_scalar(tmp[:, c, :], tmp[:, c, :], 0.0, 1.0, ALU.max, ALU.min).then_inc(s["y_step"], 1)
                        dve.wait_ge(s["y_step"], 1 + 2 * (CI * b + c) + 1)
                        dve.tensor_tensor(tmp[:, c, :], tmp[:, c, :], batch(zb, c, b), ALU.mult).then_inc(s["y_step"], 1)
                        dve.wait_ge(s["y_step"], 1 + 2 * (CI * b + c) + 2)
                        dve.tensor_scalar(yg[:, c, :], tmp[:, c, :], 0.0, 1.0, ALU.max, ALU.min).then_inc(s["yg_done"], 1)
                    dve.wait_ge(s["out_full"], 1 + b + 1)
                    dve.tensor_tensor(tokens(k.X, b), tokens(k.X, b), psum[:, 6, :], ALU.add).then_inc(s["out_done"], 1)

            @block.gpsimd
            def _(pool):
                with pool.Fori(0, B) as b:
                    for n in range(DS):
                        for c in range(CI):
                            i = CI * n + c
                            m = CI * DS * b + i
                            pool.wait_ge(s["scanned"], 1 + m + 1)
                            pool.wait_ge(s["c_copied"], 1 + DS * b + n + 1)
                            if i >= 4:
                                pool.wait_ge(s["y_full"], 1 + m - 3)
                            else:
                                pool.wait_ge(s["y_full"], 1 + CI * DS * b)
                            pool.tensor_tensor(hc[:, i % 4, :], hs[:, i % 4, :], c_sb[:, n % 2, :], ALU.mult).then_inc(s["hc_done"], 1)


def tokens(x, b):
    return x[:, ds(b, 1), PAD:ROW].rearrange("p o n -> p (o n)")


def batch(x, c, b):
    return x[:, c, ds(b, 1), :].rearrange("p o n -> p (o n)")


def batch3(x, b, rows=XD):
    return x[0:rows, ds(b, 1), :].rearrange("p o n -> p (o n)")



KEYS = MEM + N


def topk_phase(k, a):
    nc = k.nc
    psum = k.psum
    with ExitStack() as ctx:
        s = names(ctx, "tk", nc, "w_in", "mem_turned", "mem_copied", "scaled", "staged", "proj_full", "proj_evac", "qs_done", "dots", "m8", "removed",
                  "neg_top", "e_done", "p_done", "pt_full", "pt_evac", "pv_full", "rden", "o_done", "ot_full", "ot_evac", "y_full", "y_done", "scrap")

        def sb(name, shape, dt=F32):
            return ctx.enter_context(nc.sbuf_tensor(f"tk_{name}", shape, dt))

        wq = sb("wq", [P, INNER])
        wkv = sb("wkv", [P, 2 * INNER])
        wout = sb("wout", [P, PAIRS, D])
        bout = sb("bout", [P, 1])
        mix = sb("mix", [P, PAIRS, H])
        mk = sb("mk", [MEM, H, DH])
        hb = sb("hb", [P, N])
        qT = sb("qT", [P, PAIRS, N])
        kT = sb("kT", [P, PAIRS, KEYS])
        v = sb("v", [P, TILES, H, DH + 1])
        mv = sb("mv", [MEM, H, DH + 1])
        qs = sb("qs", [P, 2, PAIRS, P])
        work = sb("work", [P, KEYS])
        m8 = sb("m8", [P, 2, TOPK])
        neg_top = sb("neg_top", [P, 2, 1])
        e = sb("e", [P, 2, KEYS])
        pT = sb("pT", [P, 2, TILES + 1, P])
        rden = sb("rden", [P, 2, 1])
        o_tok = sb("o_tok", [P, H, DH])
        oT = sb("oT", [P, PAIRS, P])

        ROUNDS = TOPK // 8

        with nc.Block() as block:
            @block.sync
            def _(sp):
                sp.dma_start(wq[:, :], a["Wq"]).then_inc(s["w_in"], 16)
                sp.dma_start(wkv[:, :], a["Wkv"]).then_inc(s["w_in"], 16)
                sp.dma_start(wout[:, :, :], a["Wout"].rearrange("(c p) d -> p c d", p=P)).then_inc(s["w_in"], 16)
                sp.dma_start(bout[:, :], a["bout"].rearrange("(p o) -> p o", o=1), allow_slow_non_contiguous=True).then_inc(s["w_in"], 16)
                pre = a["pre_proj"].rearrange("(c r) k -> r c k", r=2)
                for r in range(2):
                    sp.dma_start(mix[DH * r:DH * (r + 1), :, :], pre[r, :, :].partition_broadcast(DH)).then_inc(s["w_in"], 16)
                sp.dma_start(mk[:, :, :], a["mem_k"].rearrange("h m e -> m h e")).then_inc(s["w_in"], 16)
                sp.dma_start(mv[:, :, 0:DH], a["mem_v"].rearrange("h m e -> m h e")).then_inc(s["w_in"], 16)

            @block.tensor
            def _(pe):
                pe.wait_ge(s["w_in"], 1 + 16 * 8)
                for c in range(PAIRS):
                    last = pe.transpose(psum[:, 0, MEM * c:MEM * (c + 1)], mk[:, 2 * c:2 * c + 2, :].rearrange("m h e -> m (h e)"),
                                        k.ident[0:MEM, 0:MEM])
                last.then_inc(s["mem_turned"], 1)

            @block.vector
            def _(dve):
                dve.wait_ge(s["w_in"], 1 + 16 * 8)
                dve.tensor_scalar(mix[:, :, :], mix[:, :, :], DH ** -0.5, None, ALU.mult)
                dve.memset(v[:, :, :, DH:DH + 1], 1.0)
                dve.memset(mv[:, :, DH:DH + 1], 1.0)
                dve.wait_ge(s["mem_turned"], 1 + 1)
                dve.tensor_copy(kT[:, :, 0:MEM], psum[:, 0, 0:MEM * PAIRS].rearrange("p (c m) -> p c m", m=MEM))

        UNITS = H * TILES

        def for_heads(eng, body, last=None):
            for j in range(2):
                body(True, 0, j)
            with eng.Fori(1, H // 2) as kk:
                for j in range(2):
                    body(False, kk, j)

        with nc.Block() as block:
            @block.tensor
            def _(pe):
                with pe.Fori(0, B) as b:
                    pe.wait_ge(s["staged"], 1 + b + 1)
                    for i in range(24):
                        pe.wait_ge(s["proj_evac"], 1 + 24 * b + (i - 1 if i >= 2 else 0))
                        bank = psum[:, i % 2, :]
                        if i < 8:
                            pe.matmul(bank, wq[:, P * i:P * (i + 1)], hb[:, :], start=True, stop=True).then_inc(s["proj_full"], 1)
                        elif i < 16:
                            pe.matmul(bank, wkv[:, P * (i - 8):P * (i - 7)], hb[:, :], start=True, stop=True).then_inc(s["proj_full"], 1)
                        else:
                            t, half = (i - 16) // 2, i % 2
                            pe.matmul(bank, hb[:, P * t:P * (t + 1)], wkv[:, INNER + 512 * half:INNER + 512 * (half + 1)],
                                      start=True, stop=True).then_inc(s["proj_full"], 1)
                    pe.wait_ge(s["proj_evac"], 1 + 24 * b + 24)
                    for t in range(TILES):
                        n = MEM + P * (t + 1)
                        base = UNITS * b + H * t

                        def dots(first, kk, j):
                            g = base + 2 * kk + j
                            pe.wait_ge(s["qs_done"], 1 + g + 1)
                            if not (first and t == 0):
                                pe.wait_ge(s["p_done"], 1 + g - 1)
                            else:
                                pe.wait_ge(s["p_done"], 1 + UNITS * b)
                            for lo, hi in ((0, min(n, 512)), (512, n)):
                                if lo >= hi:
                                    continue
                                bank = psum[:, 2 * j + lo // 512, 0:hi - lo]
                                d0 = n - P
                                for c in range(PAIRS):
                                    last = pe.matmul(bank, qs[:, j, c, :], kT[:, c, lo:hi], start=(c == 0), stop=False, skip_group_check=True)
                                m0, m1 = max(lo, d0), hi
                                last = pe.matmul(psum[:, 2 * j + lo // 512, m0 - lo:m1 - lo], k.ident_bf[:, :], k.causal[:, m0 - d0:m1 - d0],
                                                 start=False, stop=True, skip_group_check=True)
                            last.then_inc(s["dots"], 1)

                        def values(first, kk, j):
                            g = base + 2 * kk + j
                            pe.wait_ge(s["p_done"], 1 + g + 1)
                            if g is not None and not (first and t == 0 and j == 0):
                                pe.wait_ge(s["pt_evac"], 1 + g)
                            for i in range(t + 2):
                                lo, m = (0, MEM) if i == 0 else (MEM + P * (i - 1), P)
                                last = pe.transpose(psum[0:m, 4 + i // 4, P * (i % 4):P * (i % 4 + 1)], e[:, j, lo:lo + m], k.ident[:, :])
                            last.then_inc(s["pt_full"], 1)
                            pe.wait_ge(s["pt_evac"], 1 + g + 1)
                            pe.wait_ge(s["o_done"], 1 + g)
                            for i in range(t + 2):
                                h = j if first else ds(2 * kk + j, 1)
                                if i == 0:
                                    src = mv[:, h, :] if first else mv[:, h, :].rearrange("p o e -> p (o e)")
                                else:
                                    src = v[:, i - 1, h, :] if first else v[:, i - 1, h, :].rearrange("p o e -> p (o e)")
                                last = pe.matmul(psum[:, 6, 0:DH + 1], pT[0:(MEM if i == 0 else P), j, i, :], src, start=(i == 0), stop=(i == t + 1))
                            last.then_inc(s["pv_full"], 1)

                        dots(True, 0, 0)
                        dots(True, 0, 1)
                        values(True, 0, 0)
                        with pe.Fori(1, H // 2) as kk:
                            dots(False, kk, 0)
                            values(False, kk - 1, 1)
                            dots(False, kk, 1)
                            values(False, kk, 0)
                        values(False, H // 2 - 1, 1)
                        pe.wait_ge(s["o_done"], 1 + base + H)
                        pe.wait_ge(s["y_done"], 1 + TILES * b + t)
                        for half in range(2):
                            for c in range(4):
                                hh = 8 * half + 2 * c
                                last = pe.transpose(psum[:, 4 + half, P * c:P * (c + 1)], o_tok[:, hh:hh + 2, :].rearrange("p h e -> p (h e)"), k.ident[:, :])
                            last.then_inc(s["ot_full"], 1)
                        pe.wait_ge(s["ot_evac"], 1 + 2 * (TILES * b + t) + 2)
                        for c in range(PAIRS):
                            last = pe.matmul(psum[:, 7, 0:P], wout[:, c, :], oT[:, c, :], start=(c == 0), stop=(c == PAIRS - 1))
                        last.then_inc(s["y_full"], 1)

            @block.scalar
            def _(act):
                with act.Fori(0, B) as b:
                    for i in range(24):
                        act.wait_ge(s["proj_full"], 1 + 24 * b + i + 1)
                        src = psum[:, i % 2, :]
                        if i < 8:
                            act.activation(qT[:, i, :], src, ACT.Copy).then_inc(s["proj_evac"], 1)
                        elif i < 16:
                            act.activation(kT[:, i - 8, MEM:KEYS], src, ACT.Copy).then_inc(s["proj_evac"], 1)
                        else:
                            t, half = (i - 16) // 2, i % 2
                            act.activation(v[:, t, 8 * half:8 * half + 8, 0:DH], src.rearrange("p (h e) -> p h e", e=DH), ACT.Copy).then_inc(s["proj_evac"], 1)
                    for t in range(TILES):
                        n = MEM + P * (t + 1)
                        base = UNITS * b + H * t

                        def soft(first, kk, j):
                            g = base + 2 * kk + j
                            act.wait_ge(s["removed"], 1 + (ROUNDS - 1) * g + 1)
                            if first and t == 0:
                                act.wait_ge(s["pt_full"], 1 + UNITS * b)
                            else:
                                act.wait_ge(s["pt_full"], 1 + g - 1)
                            for lo, hi in ((0, min(n, 512)), (512, n)):
                                if lo < hi:
                                    last = act.activation(e[:, j, lo:hi], psum[:, 2 * j + lo // 512, 0:hi - lo], ACT.Exp, bias=neg_top[:, j, :])
                            last.then_inc(s["e_done"], 1)

                        def after(first, kk, j):
                            g = base + 2 * kk + j
                            act.wait_ge(s["pt_full"], 1 + g + 1)
                            act.wait_ge(s["o_done"], 1 + g)
                            act.activation(pT[0:MEM, j, 0, :], psum[0:MEM, 4, 0:P], ACT.Copy)
                            last = act.activation(pT[:, j, 1:min(t + 2, 4), :], psum[:, 4, P:P * min(t + 2, 4)].rearrange("p (i n) -> p i n", n=P), ACT.Copy)
                            if t == 3:
                                last = act.activation(pT[:, j, 4, :], psum[:, 5, 0:P], ACT.Copy)
                            last.then_inc(s["pt_evac"], 1)
                            wait_alone(act, s["rden"], g + 1, s["scrap"])
                            h = j if first else ds(2 * kk + j, 1)
                            out = o_tok[:, h, :] if first else o_tok[:, h, :].rearrange("p o e -> p (o e)")
                            act.activation(out, psum[:, 6, 0:DH], ACT.Copy, scale=rden[:, j, :]).then_inc(s["o_done"], 1)

                        soft(True, 0, 0)
                        soft(True, 0, 1)
                        if t == 0:
                            act.wait_ge(s["ot_full"], 1 + 2 * TILES * b)
                        else:
                            act.wait_ge(s["ot_full"], 1 + 2 * (TILES * b + t))
                        after(True, 0, 0)
                        with act.Fori(1, H // 2) as kk:
                            soft(False, kk, 0)
                            after(False, kk - 1, 1)
                            soft(False, kk, 1)
                            after(False, kk, 0)
                        after(False, H // 2 - 1, 1)
                        for half in range(2):
                            act.wait_ge(s["ot_full"], 1 + 2 * (TILES * b + t) + half + 1)
                            act.activation(oT[:, 4 * half:4 * half + 4, :].rearrange("p c t -> p (c t)"), psum[:, 4 + half, :], ACT.Copy).then_inc(s["ot_evac"], 1)

            @block.vector
            def _(dve):
                with dve.Fori(0, B) as b:
                    dve.wait_ge(s["proj_full"], 1 + 24 * b)
                    dve.tensor_copy(hb[:, :], tokens(k.XA, b)).then_inc(s["staged"], 1)
                    for t in range(TILES):
                        n = MEM + P * (t + 1)
                        base = UNITS * b + H * t

                        def head(first, kk, j):
                            g = base + 2 * kk + j
                            scores = psum[:, 2 * j:2 * j + 2, :].rearrange("p a n -> p (a n)")[:, 0:n]
                            wait_alone(dve, s["dots"], g + 1, s["scrap"])
                            for r in range(ROUNDS):
                                src = scores if r == 0 else work[:, 0:n]
                                if r:
                                    wait_alone(dve, s["removed"], (ROUNDS - 1) * g + r, s["scrap"])
                                dve.max(m8[:, j, 8 * r:8 * r + 8], src).then_inc(s["m8"], 1)
                                wait_alone(dve, s["m8"], ROUNDS * g + r + 1, s["scrap"])
                                if r == 0:
                                    dve.tensor_scalar(neg_top[:, j, :], m8[:, j, 0:1], -1.0, None, ALU.mult).then_inc(s["neg_top"], 1)
                                if r < ROUNDS - 1:
                                    dve.match_replace(work[:, 0:n], m8[:, j, 8 * r:8 * r + 8], src, REMOVED).then_inc(s["removed"], 1)
                            dve.wait_ge(s["e_done"], 1 + g + 1)
                            dve.scalar_tensor_tensor(e[:, j, 0:n], scores, m8[:, j, TOPK - 1:TOPK], e[:, j, 0:n], ALU.is_ge, ALU.mult).then_inc(s["p_done"], 1)

                        def recip(first, kk, j):
                            g = base + 2 * kk + j
                            dve.wait_ge(s["pv_full"], 1 + g + 1)
                            dve.reciprocal(rden[:, j, :], psum[:, 6, DH:DH + 1]).then_inc(s["rden"], 1)

                        head(True, 0, 0)
                        head(True, 0, 1)
                        recip(True, 0, 0)
                        with dve.Fori(1, H // 2) as kk:
                            head(False, kk, 0)
                            recip(False, kk - 1, 1)
                            head(False, kk, 1)
                            recip(False, kk, 0)
                        recip(False, H // 2 - 1, 1)
                        dve.wait_ge(s["y_full"], 1 + TILES * b + t + 1)
                        xt = k.X[:, ds(b, 1), PAD + P * t:PAD + P * (t + 1)].rearrange("p o n -> p (o n)")
                        dve.scalar_tensor_tensor(xt, psum[:, 7, 0:P], bout[:, 0:1], xt, ALU.add, ALU.add).then_inc(s["y_done"], 1)

            @block.gpsimd
            def _(pool):
                with pool.Fori(0, B) as b:
                    for t in range(TILES):
                        base = UNITS * b + H * t
                        if t == 0:
                            pool.wait_ge(s["proj_evac"], 1 + 24 * b + 24)

                        def scale(first, kk, j):
                            g = base + 2 * kk + j
                            if first and t == 0:
                                pool.wait_ge(s["dots"], 1 + UNITS * b)
                            else:
                                pool.wait_ge(s["dots"], 1 + g - 1)
                            h = slice(j, j + 1) if first else ds(2 * kk + j, 1)
                            pool.tensor_tensor(qs[:, j, :, :], qT[:, :, P * t:P * (t + 1)], mix[:, :, h].to_broadcast([P, PAIRS, P]), ALU.mult).then_inc(s["qs_done"], 1)

                        for_heads(pool, scale)



def build(nc, a, out):
    with ExitStack() as ctx:
        def sb(name, shape, dt=F32):
            return ctx.enter_context(nc.sbuf_tensor(name, shape, dt))

        k = Kit()
        k.nc = nc
        k.psum = ctx.enter_context(nc.psum_tensor("psum", [P, 8, 512], F32))
        k.X, k.XA, k.XB = (sb(name, [P, B, ROW]) for name in ("X", "XA", "XB"))
        k.ident, k.ident_bf, k.mean_w = sb("ident", [P, P]), sb("ident_bf", [P, P], BF16), sb("mean_w", [P, P])
        k.mask_f, k.causal, k.band = sb("mask_f", [P, P]), sb("causal", [P, P], BF16), sb("band", [P, 2, 8, 2 * WIN], BF16)
        k.eps, k.one, k.magic = sb("eps", [P, 1]), sb("one", [P, 1]), sb("magic", [P, 2 * H], U32)
        k.b1, k.b2 = sb("b1", [P, DEPTH, 2, 3]), sb("b2", [P, DEPTH])
        k.ln_g, k.ln_b = sb("ln_g", [P, DEPTH]), sb("ln_b", [P, DEPTH])
        k.rot_base, k.qk_gain = sb("rot_base", [P, 4, TILES, DH]), sb("qk_gain", [P, 2, DEPTH, DH])
        load_phase(k, a)
        norm_phase(k, "n0")
        mamba_phase(k, a)
        norm_phase(k, "n1")
        ffn_stack(k, a, "f0")
        add_phase(k, "a0")
        norm_phase(k, "n2")
        topk_phase(k, a)
        norm_phase(k, "n3")
        ffn_stack(k, a, "f1")
        add_phase(k, "a1")
        store_phase(k, out)


_INS = {"x": "L0_attn_a_hidden_states", "W_in": "L0_attn_a_W_in", "conv_w": "L0_attn_a_conv_w", "conv_b": "L0_attn_a_conv_b",
        "W_x": "L0_attn_a_W_x", "W_dt": "L0_attn_a_W_dt", "b_dt": "L0_attn_a_b_dt", "W_out": "L0_attn_a_W_out",
        "A_log": "L0_attn_a_A_log", "D": "L0_attn_a_D", "Wq": "L0_attn_b_Wq", "Wkv": "L0_attn_b_Wkv",
        "pre_proj": "L0_attn_b_pre_proj", "mem_k": "L0_attn_b_mem_k", "mem_v": "L0_attn_b_mem_v", "Wout": "L0_attn_b_Wout",
        "bout": "L0_attn_b_bout", "Wqkv": "L0_ffn_Wqkv", "q_scale": "L0_ffn_q_scale", "k_scale": "L0_ffn_k_scale", "Wo": "L0_ffn_Wo",
        "ln_g": "L0_ffn_ln_g", "ln_b": "L0_ffn_ln_b", "W1": "L0_ffn_W1", "b1": "L0_ffn_b1", "W2": "L0_ffn_W2", "b2": "L0_ffn_b2"}


def kernel(**inputs):
    import concourse.bacc as bacc
    from concourse.bass_utils import run_bass_kernel_spmd

    nc = bacc.Bacc("TRN2", target_bir_lowering=False, num_devices=1)
    arrays, args = {}, {}
    for name, given in _INS.items():
        arrays[f"in_{name}"] = np.ascontiguousarray(inputs[given])
    arrays["in_rot"] = rotary_tables()
    for key, v in arrays.items():
        args[key[3:]] = nc.dram_tensor(key, v.shape, mybir.dt.from_np(v.dtype), kind="ExternalInput").ap()
    out = nc.dram_tensor("out", (B, N, D), F32, kind="ExternalOutput").ap()
    build(nc, args, out)
    r = run_bass_kernel_spmd(nc, [arrays], core_ids=[0])
    return r.results[0]["out"]
```

```python
from contextlib import ExitStack

import concourse.bass as bass
import numpy as np
from concourse import mybir

ALU = mybir.AluOpType
ACT = mybir.ActivationFunctionType
AX_X = mybir.AxisListType.X
F32 = mybir.dt.float32
BF16 = mybir.dt.bfloat16
U32 = mybir.dt.uint32
ds = bass.ds

P = 128
B, N, D = 4, 512, 128
H, DH = 16, 64
INNER = H * DH
WIN = 32
DEPTH = LAYERS = 6
HID = 341
PAD = WIN + 1
ROW = PAD + N
TILES = N // P
LT = B * TILES
PAIRS = H // 2
WPT = P // WIN
QK_SCALE = 8.0
EPS = 1e-5
MEM = 16
TOPK = 64
DI, DS, DC, DR = 256, 16, 4, 8
CI = DI // P
XD = DR + 2 * DS
MASKED = -3.0e38
REMOVED = -3.4e38
MAGIC = 0x5F3759DF
NEWTON = 11
HCH = [(0, 128), (128, 128), (256, 85)]


def rotary_tables():
    half = np.arange(0, DH, 2, dtype=np.float32)
    inv_freq = (np.float32(1.0) / np.float32(10000.0) ** (half / np.float32(DH))).astype(np.float32)
    t = np.arange(N, dtype=np.float32)
    freqs = t[:, None] * inv_freq[None, :]
    freqs = np.concatenate([freqs, freqs], -1)
    base = (half + np.float32(0.4 * DH)) / np.float32(1.4 * DH)
    power = (t - N // 2) / np.float32(WIN // 2)
    scale = base[None, :] ** power[:, None]
    scale = np.concatenate([scale, scale], -1).astype(np.float32)
    cos, sin = np.cos(freqs), np.sin(freqs)
    sign = np.where(np.arange(DH) < DH // 2, -1.0, 1.0).astype(np.float32)[None, :]
    inv = np.float32(1.0) / scale
    return np.stack([cos * scale * QK_SCALE, cos * inv, sign * sin * scale * QK_SCALE, sign * sin * inv]).astype(np.float32)


class Kit:
    pass


def names(ctx, phase, nc, *which):
    made = {w: ctx.enter_context(nc.semaphore(f"{phase}_{w}")) for w in which}
    with nc.Block() as block:
        @block.sync
        def _(sp):
            for sem in made.values():
                sp.sem_inc(sem, 1)

    def clear():
        with nc.Block() as block:
            @block.sync
            def _(sp):
                for sem in made.values():
                    sp.sem_clear(sem)

    ctx.callback(clear)
    return made


def wait_alone(eng, sem, value, scrap):
    eng.wait_ge(sem, 1 + value)
    eng.sem_inc(scrap, 1)



LN_SEMS = ("ln_mean", "ln_centred", "ln_squared", "ln_var", "ln_sd", "ln_recip", "ln_wide", "ln_scaled", "ln_done")
LN_STAGES = B + 2


def ln_tensor(pe, k, s, src, base, ready):
    for stage in range(LN_STAGES):
        b = stage
        if b < B:
            ready(b)
            if b >= 2:
                pe.wait_ge(s["ln_centred"], 1 + base + b - 1)
            pe.matmul(k.psum[:, b % 2, :], k.mean_w[:, :], src(b), start=True, stop=True).then_inc(s["ln_mean"], 1)
        b = stage - 1
        if 0 <= b < B:
            pe.wait_ge(s["ln_squared"], 1 + base + b + 1)
            if b >= 2:
                pe.wait_ge(s["ln_sd"], 1 + base + b - 1)
            for g in range(TILES):
                last = pe.matmul(k.psum[WIN * g:WIN * (g + 1), 2 + b % 2, 0:P], k.mean_w[:, 0:WIN], k.ln_sq[:, b % 2, P * g:P * (g + 1)],
                                 start=True, stop=True)
            last.then_inc(s["ln_var"], 1)
        b = stage - 2
        if b >= 0:
            pe.wait_ge(s["ln_recip"], 1 + base + b + 1)
            if b >= 2:
                pe.wait_ge(s["ln_scaled"], 1 + base + b - 1)
            for g in range(TILES):
                last = pe.matmul(k.psum[:, 6 + b % 2, P * g:P * (g + 1)], k.row_w[:, g, :], k.ln_std[:, b % 2, :], start=True, stop=True)
            last.then_inc(s["ln_wide"], 1)


def ln_scalar(act, k, s, dst, base):
    for b in range(B + 1):
        if b < B:
            act.wait_ge(s["ln_centred"], 1 + base + b + 1)
            if b >= 2:
                act.wait_ge(s["ln_var"], 1 + base + b - 1)
            act.activation(k.ln_sq[:, b % 2, :], dst(b), ACT.Square).then_inc(s["ln_squared"], 1)
        if b >= 1:
            act.wait_ge(s["ln_var"], 1 + base + b)
            if b >= 3:
                act.wait_ge(s["ln_wide"], 1 + base + b - 2)
            act.activation(k.ln_std[:, (b - 1) % 2, :], k.psum[:, 2 + (b - 1) % 2, 0:P], ACT.Sqrt,
                           bias=k.eps[:, 0:1]).then_inc(s["ln_sd"], 1)


def ln_vector(dve, k, s, src, dst, base, gain=None, shift=None):
    for stage in range(LN_STAGES):
        b = stage
        if b < B:
            dve.wait_ge(s["ln_mean"], 1 + base + b + 1)
            dve.tensor_tensor(dst(b), src(b), k.psum[:, b % 2, :], ALU.subtract).then_inc(s["ln_centred"], 1)
        b = stage - 1
        if 0 <= b < B:
            std = k.ln_std[:, b % 2, :]
            dve.wait_ge(s["ln_sd"], 1 + base + b + 1)
            dve.reciprocal(std, std).then_inc(s["ln_recip"], 1)
        b = stage - 2
        if b >= 0:
            dve.wait_ge(s["ln_wide"], 1 + base + b + 1)
            dve.tensor_tensor(dst(b), dst(b), k.psum[:, 6 + b % 2, :], ALU.mult).then_inc(s["ln_scaled"], 1)
            if gain is not None:
                dve.wait_ge(s["ln_scaled"], 1 + base + b + 1)
                dve.tensor_scalar(dst(b), dst(b), gain, shift, ALU.mult, ALU.add).then_inc(s["ln_done"], 1)


def norm_phase(k, phase):
    nc = k.nc
    src = lambda b: k.X[:, b, PAD:ROW]
    dst = lambda b: k.XA[:, b, PAD:ROW]
    with ExitStack() as ctx:
        s = names(ctx, phase, nc, *LN_SEMS)
        k.ln_sq = ctx.enter_context(nc.sbuf_tensor(f"{phase}_ln_sq", [P, 2, N], F32))
        k.ln_std = ctx.enter_context(nc.sbuf_tensor(f"{phase}_ln_std", [P, 2, P], F32))
        with nc.Block() as block:
            @block.tensor
            def _(pe):
                ln_tensor(pe, k, s, src, 0, lambda b: None)

            @block.scalar
            def _(act):
                ln_scalar(act, k, s, dst, 0)

            @block.vector
            def _(dve):
                ln_vector(dve, k, s, src, dst, 0)



def load_phase(k, a):
    nc = k.nc
    x_rows = a["x"].rearrange("b (t p) d -> p (b t) d", p=P)
    small = lambda i, m: k.psum[0:m, 4, DEPTH * i:DEPTH * (i + 1)]
    with ExitStack() as ctx:
        s = names(ctx, "load", nc, "x_in", "small_in", "zeroed", "built", "turned", "copied")
        x_tok = ctx.enter_context(nc.sbuf_tensor("x_tok", [P, LT, P], F32))
        b1_rows = ctx.enter_context(nc.sbuf_tensor("b1_rows", [DEPTH, 2 * HID], F32))
        d_rows = ctx.enter_context(nc.sbuf_tensor("d_rows", [DEPTH, 3, D], F32))
        block = ctx.enter_context(nc.Block())

        @block.sync
        def _(sp):
            sp.dma_start(x_tok[:, :, :], x_rows).then_inc(s["x_in"], 16)
            sp.dma_start(b1_rows[:, :], a["b1"]).then_inc(s["small_in"], 16)
            for i, v in enumerate((a["b2"], a["ln_g"], a["ln_b"])):
                sp.dma_start(d_rows[:, i, :], v).then_inc(s["small_in"], 16)
            sp.dma_start(k.rot_base[:, :, :, :], a["rot"].rearrange("c (t p) e -> p c t e", p=P)).then_inc(s["small_in"], 16)
            sp.dma_start(k.qk_gain[:, 0, :, :], a["q_scale"].partition_broadcast(P)).then_inc(s["small_in"], 16)
            sp.dma_start(k.qk_gain[:, 1, :, :], a["k_scale"].partition_broadcast(P)).then_inc(s["small_in"], 16)
            sp.wait_ge(s["small_in"], 1 + 16 * 7)

        @block.gpsimd
        def _(pool):
            pool.memset(k.ident[:, :], 0.0).then_inc(s["zeroed"], 1)
            pool.memset(k.mask_f[:, :], 0.0).then_inc(s["zeroed"], 1)
            pool.wait_ge(s["zeroed"], 1 + 2)
            pool.affine_select(out=k.ident[:, :], in_=k.ident[:, :], compare_op=ALU.not_equal, fill=1.0, base=0,
                               pattern=[[-1, P]], channel_multiplier=1).then_inc(s["built"], 1)
            pool.memset(k.mean_w[:, :], 1.0 / D).then_inc(s["built"], 1)
            pool.memset(k.eps[:, :], EPS).then_inc(s["built"], 1)
            pool.memset(k.one[:, :], 1.0).then_inc(s["built"], 1)
            pool.affine_select(out=k.mask_f[:, 0:P], in_=k.mask_f[:, 0:P], compare_op=ALU.is_ge, fill=MASKED, base=0,
                               pattern=[[-1, P]], channel_multiplier=1).then_inc(s["built"], 1)
            pool.wait_ge(s["built"], 1 + 5)
            pool.tensor_copy(k.ident_bf[:, :], k.ident[:, :]).then_inc(s["built"], 1)
            pool.tensor_copy(k.causal[:, :], k.mask_f[:, 0:P]).then_inc(s["built"], 1)
            band = k.mask_f[:, 0:2 * WIN]
            pool.wait_ge(s["built"], 1 + 7)
            pool.memset(band, 0.0).then_inc(s["built"], 1)
            for w in range(WPT):
                rows = slice(WIN * w, WIN * (w + 1))
                part = k.mask_f[rows, 0:2 * WIN]
                pool.wait_ge(s["built"], 1 + 8 + 2 * w)
                pool.affine_select(out=part, in_=part, compare_op=ALU.is_ge, fill=MASKED, base=0,
                                   pattern=[[1, 2 * WIN]], channel_multiplier=-1).then_inc(s["built"], 1)
                pool.wait_ge(s["built"], 1 + 9 + 2 * w)
                pool.affine_select(out=part, in_=part, compare_op=ALU.is_ge, fill=MASKED, base=WIN,
                                   pattern=[[-1, 2 * WIN]], channel_multiplier=1).then_inc(s["built"], 1)
            for m in range(2):
                if m:
                    pool.wait_ge(s["built"], 1 + 17)
                    pool.memset(k.mask_f[0:WIN, 0:WIN], MASKED).then_inc(s["built"], 1)
                pool.wait_ge(s["built"], 1 + 16 + 2 * m)
                pool.tensor_copy(k.band[:, m, :, :], band.unsqueeze(1).to_broadcast([P, 8, 2 * WIN])).then_inc(s["built"], 1)

        @block.vector
        def _(dve):
            dve.memset(k.XA[:, :, :], 0.0)
            dve.memset(k.XB[:, :, :], 0.0)
            dve.memset(k.magic[:, :], MAGIC + 1)
            dve.wait_ge(s["built"], 1 + 1)
            for g in range(TILES):
                dve.tensor_copy(k.row_w[:, g, :], k.ident[:, WIN * g:WIN * g + 1].to_broadcast([P, P]))
            for u in range(4):
                dve.wait_ge(s["turned"], 1 + u + 1)
                dve.tensor_copy(k.X[:, u, PAD:ROW], k.psum[:, u, :]).then_inc(s["copied"], 1)
            dve.wait_ge(s["turned"], 1 + 5)
            for which in range(2):
                for c, (h0, m) in enumerate(HCH):
                    dve.tensor_copy(k.b1[0:m, :, which, c], small(which * 3 + c, m))
            for i, t in enumerate((k.b2, k.ln_g, k.ln_b)):
                dve.tensor_copy(t[:, :], small(6 + i, D))

        @block.tensor
        def _(pe):
            pe.wait_ge(s["x_in"], 1 + 16)
            pe.wait_ge(s["built"], 1 + 1)
            for u in range(4):
                for t in range(4):
                    last = pe.transpose(k.psum[:, u, t * P:(t + 1) * P], x_tok[:, 4 * u + t, :], k.ident[:, :])
                last.then_inc(s["turned"], 1)
            pe.wait_ge(s["small_in"], 1 + 16 * 7)
            for which in range(2):
                for c, (h0, m) in enumerate(HCH):
                    pe.transpose(small(which * 3 + c, m), b1_rows[:, which * HID + h0:which * HID + h0 + m], k.ident[0:DEPTH, 0:DEPTH])
            for i in range(3):
                last = pe.transpose(small(6 + i, D), d_rows[:, i, :], k.ident[0:DEPTH, 0:DEPTH])
            last.then_inc(s["turned"], 1)


def store_phase(k, out):
    nc = k.nc
    rows = out.rearrange("b (t p) d -> p b t d", p=P)
    with ExitStack() as ctx:
        s = names(ctx, "store", nc, "turned", "copied", "stored")
        y_tok = ctx.enter_context(nc.sbuf_tensor("y_tok", [P, B, TILES, P], F32))
        block = ctx.enter_context(nc.Block())

        @block.tensor
        def _(pe):
            for b in range(B):
                for t in range(TILES):
                    last = pe.transpose(k.psum[:, b, t * P:(t + 1) * P], k.X[:, b, PAD + t * P:PAD + (t + 1) * P], k.ident[:, :])
                last.then_inc(s["turned"], 1)

        @block.vector
        def _(dve):
            for b in range(B):
                dve.wait_ge(s["turned"], 1 + b + 1)
                dve.tensor_copy(y_tok[:, b, :, :], k.psum[:, b, :].rearrange("p (t d) -> p t d", t=TILES)).then_inc(s["copied"], 1)

        @block.sync
        def _(sp):
            for b in range(B):
                sp.wait_ge(s["copied"], 1 + b + 1)
                sp.dma_start(rows[:, b, :, :], y_tok[:, b, :, :]).then_inc(s["stored"], 16)
            sp.wait_ge(s["stored"], 1 + 16 * B)


def add_phase(k, phase):
    with k.nc.Block() as block:
        @block.vector
        def _(dve):
            for b in range(B):
                dve.tensor_tensor(k.X[:, b, PAD:ROW], k.X[:, b, PAD:ROW], k.XA[:, b, PAD:ROW], ALU.add)



def turn_units(kk):
    if isinstance(kk, int):
        return sum((3 <= j <= 18) + 4 * (1 <= j <= 16) + 4 * (2 <= j <= 17) for j in range(kk))
    return 9 * kk - 15


TURN_LAYER = 9 * LT
QKV_UNITS = 6
V_DMAS = 10 * 16


def ffn_stack(k, a, phase):
    nc = k.nc
    with ExitStack() as ctx:
        s = names(ctx, phase, nc, *LN_SEMS, "wqkv_in", "wo_in", "w12_in", "tabled", "zeroed", "xs_ready", "proj_full", "proj_evac", "v_in_even", "v_in_odd",
                  "sq_done", "ss_done", "newton", "rn_ready", "rope_added", "rot_done", "add_done", "t_full",
                  "t_evac", "scores", "top", "sub_done", "exp_done", "summed", "rden_done", "pv_done", "on_done",
                  "wo_done", "res_done", "shifted", "gate_full", "gate_evac", "val_full", "val_evac", "out_full", "out_evac", "scrap")

        def sb(name, shape, dt=F32):
            return ctx.enter_context(nc.sbuf_tensor(f"{phase}_{name}", shape, dt))

        wqkv = sb("wqkv", [P, 3 * INNER])
        wo = sb("wo", [P, PAIRS, D])
        w1 = sb("w1", [P, 2 * HID])
        w2 = sb("w2", [P, 3, D])
        rot = sb("rot", [P, 4, TILES, DH])
        xs = sb("xs", [P, 2, P])
        raw = sb("raw", [P, 2, H, DH])
        sq = sb("sq", [P, 2, H, DH])
        ss = sb("ss", [P, 2 * H])
        nt = sb("nt", [P, 4, 2 * H])
        rn = sb("rn", [P, 2 * H])
        rope = sb("rope", [P, 2, 2, H, DH])
        t2 = sb("t2", [P, 2, H, DH])
        qT = sb("qT", [P, PAIRS, P])
        kT = sb("kT", [P, PAIRS, 2, WIN + 2 * P])
        v_tok = sb("v_tok", [P, 2, 2, PAIRS, DH])
        v2 = sb("v2", [P, 2, WPT, 2, PAIRS, DH])
        prob = sb("prob", [P, H, 2 * WIN])
        probT = sb("probT", [P, PAIRS, P])
        top = sb("top", [P, H])
        den = sb("den", [P, H])
        rden = sb("rden", [P, 2, H])
        o_tok = sb("o_tok", [P, H, DH])
        oT = sb("oT", [P, PAIRS, P])
        wo_sb = sb("wo_sb", [P, P])
        warm = sb("warm", [P, 1])
        xn = raw[:, :, :, :].rearrange("p a h e -> p (a h e)").rearrange("p (b n) -> p b n", b=B)
        k.ln_sq = sq[:, 0, :, :].rearrange("p h e -> p (h e)").rearrange("p (i n) -> p i n", i=2)
        k.ln_std = sq[:, 1, 0:4, :].rearrange("p h e -> p (h e)").rearrange("p (i n) -> p i n", i=2)
        gate = t2[:, 0, :, :].rearrange("p h e -> p (h e)").rearrange("p (i n) -> p i n", i=2)
        hid = rope[:, :, :, :, :].rearrange("p a c h e -> p (a c h e)").rearrange("p (i c n) -> p i c n", i=2, c=4)

        psum = k.psum

        def steps(eng, fn, L):
            for j in range(4):
                fn(L, 0, j, j)
            with eng.Fori(1, B) as b:
                for j in range(4):
                    fn(L, b, j, 4 * b + j)
            for j in range(3):
                fn(L, B, j, LT + j)

        def tile(x, r0, r1, b, t0, n=P):
            if isinstance(b, int):
                return x[r0:r1, b, t0:t0 + n]
            return x[r0:r1, ds(b, 1), t0:t0 + n].rearrange("p o n -> p (o n)")

        def v_sem(slot):
            return s["v_in_even"] if slot == 0 else s["v_in_odd"]

        def on(kk, lag):
            return not isinstance(kk, int) or 0 <= kk - lag < LT

        with nc.Block() as block:
            @block.sync
            def _(sp):
                def spread_v(g, slot):
                    v_in = v_sem(slot)
                    wait_alone(sp, s["proj_evac"], QKV_UNITS * g + QKV_UNITS + 2, s["scrap"])
                    wait_alone(sp, s["pv_done"], g + 1, s["scrap"])
                    for par in range(2):
                        r0 = DH * par
                        sp.dma_start(v2[r0:r0 + WIN, slot, 0, par, :, :], v_tok[P - WIN:P, 1 - slot, par, :, :]).then_inc(v_in, 16)
                        sp.dma_start(v2[r0 + WIN:r0 + 2 * WIN, slot, 0, par, :, :], v_tok[0:WIN, slot, par, :, :]).then_inc(v_in, 16)
                        for w in range(1, WPT):
                            sp.dma_start(v2[r0:r0 + 2 * WIN, slot, w, par, :, :], v_tok[WIN * (w - 1):WIN * (w + 1), slot, par, :, :]).then_inc(v_in, 16)

                sp.sem_inc(s["pv_done"], 2)
                sp.wait_ge(s["zeroed"], 1 + 3)
                with sp.Fori(0, LAYERS) as L:
                    sp.wait_ge(s["proj_evac"], 1 + QKV_UNITS * LT * L + 2)
                    sp.dma_start(wqkv[:, :], a["Wqkv"][ds(L, 1), :, :].rearrange("l p n -> p (l n)")).then_inc(s["wqkv_in"], 16)
                    sp.wait_ge(s["wo_done"], 1 + LT * L + 1)
                    sp.dma_start(wo[:, :, :], a["Wo"][ds(L, 1), :, :].rearrange("l (c p) d -> p (l c) d", p=P)).then_inc(s["wo_in"], 16)
                    sp.wait_ge(s["out_full"], 1 + B * L + 1)
                    sp.dma_start(w1[:, :], a["W1"][ds(L, 1), :, :].rearrange("l p n -> p (l n)")).then_inc(s["w12_in"], 16)
                    for c, (h0, m) in enumerate(HCH):
                        sp.dma_start(w2[0:m, c, :], a["W2"][ds(L, 1), h0:h0 + m, :].rearrange("l p n -> p (l n)")).then_inc(s["w12_in"], 16)
                    with sp.Fori(0, LT // 2) as t:
                        for slot in range(2):
                            spread_v(LT * L + 2 * t + slot, slot)
                sp.wait_ge(s["w12_in"], 1 + 16 * 4 * LAYERS)
                for slot in range(2):
                    sp.wait_ge(v_sem(slot), 1 + V_DMAS * LAYERS * LT // 2)

            @block.tensor
            def _(pe):
                def turn_bank(kk, j, i, L):
                    u = turn_units(kk) + i
                    pe.wait_ge(s["t_evac"], 1 + TURN_LAYER * L + u + 1)
                    return 2 + (turn_units(j if isinstance(kk, int) and kk < 4 else (4 + j) if not isinstance(kk, int) else kk) + i) % 2

                def unit(L, kk, i, fill):
                    u = QKV_UNITS * (LT * L + kk) + i
                    pe.wait_ge(s["proj_evac"], 1 + u + 1)
                    fill(psum[:, i % 2, :]).then_inc(s["proj_full"], 1)

                def step(L, b, j, kk):
                    i = 0
                    p = j % 2

                    def project_qk(n):
                        if on(kk, 0):
                            unit(L, kk, n, lambda bank: pe.matmul(bank, xs[:, p, :], wqkv[:, 512 * n:512 * (n + 1)], start=True, stop=True))

                    def project_v(par):
                        if on(kk, 0):
                            heads = wqkv[:, 2 * INNER:].rearrange("p (c r e) -> p r c e", r=2, e=DH)[:, par, :, :]
                            unit(L, kk, 4 + par, lambda bank: pe.matmul(bank, xs[:, p, :], heads, start=True, stop=True))

                    def turn_prob(n):
                        bank = turn_bank(kk, j, i, L)
                        for c in range(4):
                            last = pe.transpose(psum[:, bank, c * P:(c + 1) * P],
                                                prob[:, 8 * n + 2 * c:8 * n + 2 * c + 2, :].rearrange("p h w -> p (h w)"), k.ident[:, :])
                        last.then_inc(s["t_full"], 1)

                    def turn_qk(n):
                        bank = turn_bank(kk, j, i, L)
                        for c in range(4):
                            h = 8 * (n % 2) + 2 * c
                            last = pe.transpose(psum[:, bank, c * P:(c + 1) * P],
                                                rope[:, (j - 1) % 2, n // 2, h:h + 2, :].rearrange("p h e -> p (h e)"), k.ident[:, :])
                        last.then_inc(s["t_full"], 1)

                    if on(kk, 0):
                        if isinstance(kk, int) and kk == 0:
                            pe.wait_ge(s["wqkv_in"], 1 + 16 * L + 16)
                        pe.wait_ge(s["xs_ready"], 1 + 2 * ((LT + 1) * L + kk) + 2)
                    project_qk(0)
                    if isinstance(kk, int) and kk == 0:
                        pe.wait_ge(s["out_evac"], 1 + B * L)
                    project_qk(1)
                    if on(kk, 3):
                        if isinstance(kk, int) and kk == 3:
                            pe.wait_ge(s["wo_in"], 1 + 16 * L + 16)
                        u_ot = turn_units(kk)
                        bank = turn_bank(kk, j, i, L)
                        pe.wait_ge(s["t_evac"], 1 + TURN_LAYER * L + u_ot + 2)
                        for c in range(PAIRS):
                            last = pe.matmul(psum[:, bank, 0:P], wo[:, c, :], oT[:, c, :], start=(c == 0), stop=(c == PAIRS - 1))
                        last.then_inc(s["wo_done"], 1)
                        i += 1
                    project_qk(2)
                    if on(kk, 2):
                        pe.wait_ge(s["exp_done"], 1 + LT * L + kk - 2 + 1)
                        turn_prob(0)
                        i += 1
                    project_qk(3)
                    if on(kk, 2):
                        turn_prob(1)
                        i += 1
                        pt_end = i
                    project_v(0)
                    if on(kk, 1):
                        pe.wait_ge(s["add_done"], 1 + 2 * (LT * L + kk - 1) + 1 + 2)
                        for n in range(2):
                            turn_qk(n)
                            i += 1
                    project_v(1)
                    if on(kk, 1):
                        pe.wait_ge(s["add_done"], 1 + 2 * (LT * L + kk - 1) + 2 + 2)
                        for n in (2, 3):
                            turn_qk(n)
                            i += 1
                        tqk_end = i
                    if on(kk, 2):
                        g = LT * L + kk - 2
                        pe.wait_ge(s["t_evac"], 1 + TURN_LAYER * L + turn_units(kk) + pt_end + 2)
                        tiles = (kk - 2) // 2 if isinstance(kk, int) else 2 * b + (j - 2) // 2
                        pe.wait_ge(v_sem(j % 2), 1 + V_DMAS * (LT // 2 * L + tiles + 1))
                        pe.wait_ge(s["on_done"], 1 + g + 1)
                        for w in range(WPT):
                            for c in range(PAIRS):
                                last = pe.matmul(psum[WIN * w:WIN * (w + 1), 6 + c // 4, (c % 4) * P:(c % 4 + 1) * P],
                                                 probT[:, c, WIN * w:WIN * (w + 1)], v2[:, (j - 2) % 2, w, :, c, :], start=True, stop=True)
                        last.then_inc(s["pv_done"], 1)
                    if on(kk, 1):
                        g = LT * L + kk - 1
                        sj = (j - 1) % 4
                        pe.wait_ge(s["t_evac"], 1 + TURN_LAYER * L + turn_units(kk) + tqk_end + 2)
                        pe.wait_ge(s["sub_done"], 1 + g + 1)
                        for half in range(2):
                            pe.matmul(psum[:, 4 + half, :], k.ident_bf[:, :], k.band[:, int(sj == 0), :, :].rearrange("p h w -> p (h w)"),
                                      start=True, stop=False, skip_group_check=True)
                        for w in range(WPT):
                            t0 = P * (sj % 2) + WIN * w
                            for c in range(PAIRS):
                                last = pe.matmul(psum[WIN * w:WIN * (w + 1), 4 + c // 4, (c % 4) * P:(c % 4 + 1) * P],
                                                 qT[:, c, WIN * w:WIN * (w + 1)], kT[:, c, :, t0:t0 + 2 * WIN],
                                                 start=False, stop=True, skip_group_check=True)
                        last.then_inc(s["scores"], 1)
                    if on(kk, 2):
                        pe.wait_ge(s["on_done"], 1 + LT * L + kk - 2 + 2)
                        for n in range(2):
                            bank = turn_bank(kk, j, i, L)
                            for c in range(4):
                                h = 8 * n + 2 * c
                                last = pe.transpose(psum[:, bank, c * P:(c + 1) * P],
                                                    o_tok[:, h:h + 2, :].rearrange("p h e -> p (h e)"), k.ident[:, :])
                            last.then_inc(s["t_full"], 1)
                            i += 1

                def feed_forward(L):
                    ln_tensor(pe, k, s, lambda b: xn[:, b, :], B * L, lambda b: pe.wait_ge(s["shifted"], 1 + 2 * (B * L + b) + 2))
                    pe.wait_ge(s["w12_in"], 1 + 64 * L + 64)

                    def output(b):
                        pe.wait_ge(s["val_evac"], 1 + 12 * L + 3 * b + 3)
                        if b >= 2:
                            pe.wait_ge(s["out_evac"], 1 + B * L + b - 1)
                        for c, (h0, m) in enumerate(HCH):
                            last = pe.matmul(psum[:, b % 2, :], w2[0:m, c, :], hid[0:m, b % 2, c, :], start=(c == 0), stop=(c == 2))
                        last.then_inc(s["out_full"], 1)

                    pe.wait_ge(s["ln_scaled"], 1 + B * L + B)
                    for b in range(B):
                        pe.wait_ge(s["ln_done"], 1 + B * L + b + 1)
                        for c, (h0, m) in enumerate(HCH):
                            for which in range(2):
                                n = 3 * b + c
                                full, evac = (s["gate_full"], s["gate_evac"]) if which == 0 else (s["val_full"], s["val_evac"])
                                if n >= 2:
                                    pe.wait_ge(evac, 1 + 12 * L + n - 1)
                                col = (HID if which == 0 else 0) + h0
                                pe.matmul(psum[0:m, 4 + 2 * which + n % 2, :], w1[:, col:col + m], xn[:, b, :],
                                          start=True, stop=True).then_inc(full, 1)
                            if c == 0 and b:
                                output(b - 1)
                    output(B - 1)

                with pe.Fori(0, LAYERS) as L:
                    steps(pe, step, L)
                    feed_forward(L)

            @block.scalar
            def _(act):
                act.sem_inc(s["proj_evac"], 2)
                act.sem_inc(s["t_evac"], 2)

                def step(L, b, j, kk):
                    u_t = TURN_LAYER * L + turn_units(kk)
                    i = 0

                    def evac(out, bank, source=None):
                        return act.activation(out, psum[:, bank, :] if source is None else source, ACT.Copy)

                    def t_bank(i):
                        static = turn_units(4 + j) if not isinstance(kk, int) else turn_units(kk)
                        return 2 + (static + i) % 2

                    g0 = LT * L + kk

                    def copy_qk(n):
                        if on(kk, 0):
                            act.wait_ge(s["proj_full"], 1 + QKV_UNITS * g0 + n + 1)
                            if n % 2 == 0:
                                act.wait_ge(s["rot_done"], 1 + 2 * g0 + n // 2 + 1)
                            evac(raw[:, n // 2, 8 * (n % 2):8 * (n % 2) + 8, :].rearrange("p h e -> p (h e)"), n % 2).then_inc(s["proj_evac"], 1)

                    def square(half):
                        if on(kk, 0):
                            act.wait_ge(s["proj_evac"], 1 + QKV_UNITS * g0 + 2 * half + 2 + 2)
                            act.wait_ge(s["ss_done"], 1 + 2 * g0 + half + 1)
                            act.activation(sq[:, half, :, :], raw[:, half, :, :], ACT.Square).then_inc(s["sq_done"], 1)

                    def copy_v(par):
                        if on(kk, 0):
                            if par == 0:
                                if not isinstance(kk, int) or kk >= 1:
                                    tiles = (kk - 1) // 2 if isinstance(kk, int) else 2 * b + (j - 1) // 2
                                    act.wait_ge(v_sem((j - 1) % 2), 1 + V_DMAS * (LT // 2 * L + tiles + 1))
                                else:
                                    act.wait_ge(v_sem(1), 1 + V_DMAS * (LT // 2) * L)
                            act.wait_ge(s["proj_full"], 1 + QKV_UNITS * g0 + 4 + par + 1)
                            evac(v_tok[:, j % 2, par, :, :].rearrange("p c e -> p (c e)"), par).then_inc(s["proj_evac"], 1)

                    def copy_prob(n):
                        act.wait_ge(s["t_full"], 1 + u_t_full(L, kk, i))
                        evac(probT[:, 4 * n:4 * n + 4, :].rearrange("p c t -> p (c t)"), t_bank(i)).then_inc(s["t_evac"], 1)

                    def copy_q(n):
                        act.wait_ge(s["t_full"], 1 + u_t_full(L, kk, i))
                        evac(qT[:, 4 * n:4 * n + 4, :].rearrange("p c t -> p (c t)"), t_bank(i)).then_inc(s["t_evac"], 1)

                    copy_qk(0)
                    copy_qk(1)
                    square(0)
                    if on(kk, 2):
                        act.wait_ge(s["sub_done"], 1 + g0 - 2 + 2)
                        act.activation(prob[:, :, :], prob[:, :, :], ACT.Exp).then_inc(s["exp_done"], 1)
                    if on(kk, 3):
                        act.wait_ge(s["wo_done"], 1 + g0 - 3 + 2)
                        act.wait_ge(s["res_done"], 1 + g0 - 3 + 1)
                        evac(wo_sb[:, :], 0, psum[:, t_bank(i), 0:P]).then_inc(s["t_evac"], 1)
                        i += 1
                    copy_qk(2)
                    if on(kk, 2):
                        act.wait_ge(s["pv_done"], 1 + g0 - 2 + 2)
                        copy_prob(0)
                        i += 1
                    copy_qk(3)
                    if on(kk, 2):
                        copy_prob(1)
                        i += 1
                    copy_v(0)
                    square(1)
                    if on(kk, 1):
                        act.wait_ge(s["scores"], 1 + g0 - 1)
                        for n in range(2):
                            copy_q(n)
                            i += 1
                    copy_v(1)
                    if on(kk, 1):
                        sj = (j - 1) % 4
                        slot = WIN + P * (sj % 2)
                        for n in range(2):
                            act.wait_ge(s["t_full"], 1 + u_t_full(L, kk, i))
                            turned = psum[:, t_bank(i), :].rearrange("p (c t) -> p c t", c=4)
                            for par in range(2):
                                rows = slice(DH * par, DH * (par + 1))
                                if sj == 1:
                                    evac(kT[rows, 4 * n:4 * n + 4, par, 0:WIN], 0, turned[rows, :, P - WIN:P])
                                last = evac(kT[rows, 4 * n:4 * n + 4, par, slot:slot + P], 0, turned[rows, :, :])
                            last.then_inc(s["t_evac"], 1)
                            i += 1
                    if on(kk, 2):
                        act.wait_ge(s["wo_done"], 1 + g0 - 2 + 1)
                        for n in range(2):
                            act.wait_ge(s["t_full"], 1 + u_t_full(L, kk, i))
                            evac(oT[:, 4 * n:4 * n + 4, :].rearrange("p c t -> p (c t)"), t_bank(i)).then_inc(s["t_evac"], 1)
                            i += 1
                def u_t_full(L, kk, i):
                    before = turn_units(kk) - min(max(kk - 2, 0), LT) if isinstance(kk, int) else 8 * kk - 13
                    return 8 * LT * L + before + i + 1

                with act.Fori(0, LAYERS) as L:
                    steps(act, step, L)
                    act.activation(warm[:, :], k.one[:, :], ACT.Sqrt)
                    ln_scalar(act, k, s, lambda b: xn[:, b, :], B * L)
                    act.activation(warm[:, :], k.one[:, :], ACT.Gelu)
                    for b in range(B):
                        for c, (h0, m) in enumerate(HCH):
                            n = 3 * b + c
                            if n >= 2:
                                act.wait_ge(s["val_evac"], 1 + 12 * L + n - 1)
                            wait_alone(act, s["gate_full"], 12 * L + n + 1, s["scrap"])
                            act.activation(gate[0:m, n % 2, :], psum[0:m, 4 + n % 2, :], ACT.Gelu,
                                           bias=k.b1[0:m, ds(L, 1), 1, c]).then_inc(s["gate_evac"], 1)
                    act.activation(warm[:, :], k.one[:, :], ACT.Exp)

            @block.vector
            def _(dve):
                dve.memset(kT[:, :, :, :], 0.0).then_inc(s["zeroed"], 1)
                dve.memset(v2[:, :, :, :, :, :], 0.0).then_inc(s["zeroed"], 1)
                dve.memset(v_tok[:, :, :, :, :], 0.0).then_inc(s["zeroed"], 1)
                dve.wait_ge(s["zeroed"], 1 + 3)
                for sem, n in ((s["rot_done"], 2), (s["ss_done"], 2), (s["sub_done"], 1), (s["on_done"], 1)):
                    dve.sem_inc(sem, n)

                def newton(g, between):
                    at = [0]

                    def link(ins):
                        at[0] += 1
                        ins.then_inc(s["newton"], 1)
                        if at[0] in between:
                            between[at[0]]()
                        wait_alone(dve, s["newton"], NEWTON * g + at[0], s["scrap"]) if at[0] == 2 else dve.wait_ge(s["newton"], 1 + NEWTON * g + at[0])

                    x, h, y, z = (nt[:, n, :] for n in range(4))
                    link(dve.tensor_scalar(x, ss[:, :], 1e-24, None, ALU.max))
                    link(dve.tensor_scalar(h.bitcast(U32), x.bitcast(U32), 1, 0xFFFFFFFF, ALU.logical_shift_right, ALU.bitwise_xor))
                    link(dve.tensor_tensor(y.bitcast(U32), h.bitcast(U32), k.magic[:, :], ALU.add))
                    for n in range(3):
                        link(dve.scalar_tensor_tensor(z, y, -0.5, y, ALU.mult, ALU.mult))
                        link(dve.tensor_tensor(h, z, x, ALU.mult))
                        if n == 2:
                            dve.wait_ge(s["add_done"], 1 + 2 * g + 2)
                            dve.scalar_tensor_tensor(rn[:, :], h, 1.5, y, ALU.add, ALU.mult).then_inc(s["rn_ready"], 1)
                        else:
                            link(dve.scalar_tensor_tensor(y, h, 1.5, y, ALU.add, ALU.mult))

                def shifted(L, b, j, t):
                    late = not isinstance(t, int) or t >= 2
                    dve.wait_ge(s["proj_evac"], 1 + QKV_UNITS * (LT * L + (t - 1 if late else 0)) + 2)
                    t0 = PAD + P * j
                    dve.tensor_copy(xs[0:DH, j % 2, :], tile(k.XA, 0, DH, b, t0)).then_inc(s["xs_ready"], 1)
                    dve.tensor_copy(xs[DH:P, j % 2, :], tile(k.XA, DH, P, b, t0 - 1)).then_inc(s["xs_ready"], 1)

                def rotate(g, j, half):
                    hd = DH // 2
                    dve.wait_ge(s["proj_evac"], 1 + QKV_UNITS * g + 2 * half + 2 + 2)
                    cos = rot[:, half, j, :].unsqueeze(1).to_broadcast([P, H, DH])
                    dve.tensor_tensor(rope[:, j % 2, half, :, :], raw[:, half, :, :], cos, ALU.mult)
                    dve.wait_ge(s["add_done"], 1 + 2 * g + half + 1)
                    for q in range(2):
                        sin = rot[:, 2 + half, j, hd * q:hd * (q + 1)].unsqueeze(1).to_broadcast([P, H, hd])
                        last = dve.tensor_tensor(t2[:, half, :, hd * q:hd * (q + 1)], raw[:, half, :, hd * (1 - q):hd * (2 - q)], sin, ALU.mult)
                    last.then_inc(s["rot_done"], 1)

                def step(L, b, j, kk):
                    g0 = LT * L + kk

                    def den_sum():
                        dve.wait_ge(s["exp_done"], 1 + g0 - 2 + 1)
                        dve.tensor_reduce(den[:, :], prob[:, :, :], AX_X, ALU.add).then_inc(s["summed"], 1)

                    def den_recip():
                        dve.wait_ge(s["summed"], 1 + g0 - 2 + 1)
                        dve.reciprocal(rden[:, j % 2, :], den[:, :]).then_inc(s["rden_done"], 1)

                    if on(kk, 0):
                        if isinstance(kk, int) and kk == 0:
                            dve.wait_ge(s["out_evac"], 1 + B * L)
                        if j < 3:
                            shifted(L, b, j + 1, kk + 1)
                        else:
                            shifted(L, b + 1, 0, kk + 1)
                        if isinstance(kk, int) and kk == 0:
                            tables(L)
                        if not isinstance(kk, int) or kk >= 2:
                            dve.wait_ge(s["scores"], 1 + g0 - 1)
                        rotate(g0, j, 0)
                        for half in range(2):
                            dve.wait_ge(s["sq_done"], 1 + 2 * g0 + half + 1)
                            dve.tensor_reduce(ss[:, H * half:H * (half + 1)], sq[:, half, :, :], AX_X, ALU.add).then_inc(s["ss_done"], 1)
                        dve.wait_ge(s["ss_done"], 1 + 2 * g0 + 2 + 2)
                        newton(g0, {2: den_sum, 4: den_recip} if on(kk, 2) else {})
                    elif on(kk, 2):
                        den_sum()
                        den_recip()
                    if on(kk, 2):
                        g = g0 - 2
                        dve.wait_ge(s["pv_done"], 1 + g + 1 + 2)
                        dve.wait_ge(s["rden_done"], 1 + g + 1)
                        dve.wait_ge(s["wo_done"], 1 + g + 1)
                        dve.tensor_tensor(o_tok[:, :, :], psum[:, 6:8, :].rearrange("p a n -> p (a n)").rearrange("p (h e) -> p h e", e=DH),
                                          rden[:, (j - 2) % 2, :].unsqueeze(2).to_broadcast([P, H, DH]), ALU.mult).then_inc(s["on_done"], 1)
                    if on(kk, 0):
                        rotate(g0, j, 1)
                    if on(kk, 1):
                        g = g0 - 1
                        sc = psum[:, 4:6, :].rearrange("p a n -> p (a n)").rearrange("p (h w) -> p h w", w=2 * WIN)
                        dve.wait_ge(s["scores"], 1 + g + 1)
                        dve.tensor_reduce(top[:, :], sc, AX_X, ALU.max).then_inc(s["top"], 1)
                        dve.wait_ge(s["top"], 1 + g + 1)
                        dve.wait_ge(s["pv_done"], 1 + g + 2)
                        dve.tensor_tensor(prob[:, :, :], sc, top[:, :].unsqueeze(2).to_broadcast([P, H, 2 * WIN]),
                                          ALU.subtract).then_inc(s["sub_done"], 1)

                def tables(L):
                    hd = DH // 2
                    for half in range(2):
                        gain = k.qk_gain[:, half, ds(L, 1), :]
                        dve.tensor_tensor(rot[:, half, :, :], k.rot_base[:, half, :, :], gain.to_broadcast([P, TILES, DH]), ALU.mult)
                        for q in range(2):
                            dve.tensor_tensor(rot[:, 2 + half, :, hd * q:hd * (q + 1)], k.rot_base[:, 2 + half, :, hd * q:hd * (q + 1)],
                                              k.qk_gain[:, half, ds(L, 1), hd * (1 - q):hd * (2 - q)].to_broadcast([P, TILES, hd]),
                                              ALU.mult).then_inc(s["tabled"], 1)
                    dve.wait_ge(s["tabled"], 1 + 4 * L + 4)

                def first_tile(L):
                    dve.wait_ge(s["proj_evac"], 1 + QKV_UNITS * LT * L + 2)
                    dve.tensor_copy(xs[0:DH, 0, :], k.XA[0:DH, 0, PAD:PAD + P]).then_inc(s["xs_ready"], 1)
                    dve.tensor_copy(xs[DH:P, 0, :], k.XA[DH:P, 0, PAD - 1:PAD + P - 1]).then_inc(s["xs_ready"], 1)

                first_tile(0)
                with dve.Fori(0, LAYERS) as L:
                    steps(dve, step, L)
                    for b in range(B):
                        dve.wait_ge(s["res_done"], 1 + LT * L + TILES * (b + 1) + 1)
                        dve.tensor_copy(xn[0:DH, b, :], k.XB[0:DH, b, PAD:ROW]).then_inc(s["shifted"], 1)
                        dve.tensor_copy(xn[DH:P, b, :], k.XB[DH:P, b, PAD - 1:ROW - 1]).then_inc(s["shifted"], 1)
                    ln_vector(dve, k, s, lambda b: xn[:, b, :], lambda b: xn[:, b, :], B * L,
                              k.ln_g[:, ds(L, 1)], k.ln_b[:, ds(L, 1)])

                    def output(b):
                        if b == B - 1:
                            dve.wait_ge(s["out_evac"], 1 + B * L + 1)
                            first_tile(L + 1)
                        dve.wait_ge(s["out_full"], 1 + B * L + b + 1 + 1)
                        dve.scalar_tensor_tensor(k.XA[:, b, PAD:ROW], psum[:, b % 2, :], k.b2[:, ds(L, 1)], k.XB[:, b, PAD:ROW],
                                                 ALU.add, ALU.add).then_inc(s["out_evac"], 1)

                    for b in range(B):
                        for c, (h0, m) in enumerate(HCH):
                            n = 3 * b + c
                            dve.wait_ge(s["val_full"], 1 + 12 * L + n + 1)
                            dve.wait_ge(s["gate_evac"], 1 + 12 * L + n + 1)
                            if b >= 2 and c == 0:
                                dve.wait_ge(s["out_full"], 1 + B * L + b)
                            dve.scalar_tensor_tensor(hid[0:m, b % 2, c, :], psum[0:m, 6 + n % 2, :], k.b1[0:m, ds(L, 1), 0, c],
                                                     gate[0:m, n % 2, :], ALU.add, ALU.mult).then_inc(s["val_evac"], 1)
                            if c == 1 and b:
                                output(b - 1)
                    output(B - 1)

            @block.gpsimd
            def _(pool):
                pool.sem_inc(s["wo_done"], 1)
                pool.sem_inc(s["out_full"], 1)
                pool.sem_inc(s["add_done"], 2)
                pool.sem_inc(s["res_done"], 1)

                def step(L, b, j, kk):
                    g0 = LT * L + kk
                    if on(kk, 3):
                        pool.wait_ge(s["t_evac"], 1 + TURN_LAYER * L + turn_units(kk) + 1 + 2)
                        jj, bb = (j - 3) % 4, (b if j == 3 else b - 1)
                        t0 = PAD + P * jj
                        pool.tensor_tensor(tile(k.XB, 0, P, bb, t0, P), wo_sb[:, :], tile(k.XA, 0, P, bb, t0, P), ALU.add).then_inc(s["res_done"], 1)
                    if on(kk, 0):
                        for half in range(2):
                            pool.wait_ge(s["rot_done"], 1 + 2 * g0 + half + 1 + 2)
                            part = rope[:, j % 2, half, :, :]
                            pool.tensor_tensor(part, part, t2[:, half, :, :], ALU.add).then_inc(s["rope_added"], 1)
                            pool.wait_ge(s["rope_added"], 1 + 2 * g0 + half + 1)
                            pool.wait_ge(s["rn_ready"], 1 + g0 + 1)
                            pool.tensor_tensor(part, part, rn[:, H * half:H * (half + 1)].unsqueeze(2).to_broadcast([P, H, DH]),
                                               ALU.mult).then_inc(s["add_done"], 1)

                with pool.Fori(0, LAYERS) as L:
                    steps(pool, step, L)




def mamba_phase(k, a):
    nc = k.nc
    psum = k.psum
    with ExitStack() as ctx:
        load = names(ctx, "mw", nc, "loaded", "turned", "copied", "done")
        s = names(ctx, "mb", nc, "zeroed", "xz_full", "xz_evac", "conv_in", "conv_step", "silu", "u_done", "xd_full", "xd_evac", "dt_full", "dt_in", "dt_abs",
                  "dt_exp", "dt_ln", "dt_max", "dt_done", "sel", "bc_full", "b_used", "c_copied", "da_done", "dbu", "scanned", "hc_done",
                  "y_full", "y_evac", "y_step", "yg_done", "out_full", "out_done", "staged", "copied", "scrap")

        def sb(name, shape, dt=F32):
            return ctx.enter_context(nc.sbuf_tensor(f"mb_{name}", shape, dt))

        w_inT = sb("w_inT", [P, 2 * DI])
        w_xT = sb("w_xT", [P, CI, XD])
        w_dtT = sb("w_dtT", [DR, DI])
        w_outT = sb("w_outT", [P, CI, D])
        conv_w = sb("conv_w", [P, CI, DC])
        conv_b = sb("conv_b", [P, CI])
        b_dt = sb("b_dt", [P, CI])
        skip = sb("skip", [P, CI])
        neg_a = sb("neg_a", [P, CI, DS])
        sel = sb("sel", [P, 2 * DS, P])
        w_nat = sb("w_nat", [P, 4, P])
        wx_nat = sb("wx_nat", [XD, DI])
        wdt_nat = sb("wdt_nat", [P, CI, DR])
        wo_nat = sb("wo_nat", [P, DI])
        vec_nat = sb("vec_nat", [CI, 3, P])
        xp = sb("xp", [P, CI, DC - 1 + N])
        zb = sb("zb", [P, CI, B, N])
        u = sb("u", [P, CI, B, N])
        dt = sb("dt", [P, CI, B, N])
        xd = sb("xd", [P, B, N])
        conv = sb("conv", [P, CI, N])
        dtr = sb("dtr", [DR, N])
        tmp = sb("tmp", [P, CI, N])
        dtu = sb("dtu", [P, CI, N])
        c_sb = sb("c_sb", [P, 2, N])
        da = sb("da", [P, 4, N])
        dbu = sb("dbu", [P, 4, N])
        hs = sb("hs", [P, 4, N])
        hc = sb("hc", [P, 4, N])
        yg = sb("yg", [P, CI, N])

        with nc.Block() as block:
            @block.sync
            def _(sp):
                sp.dma_start(w_nat[:, :, :], a["W_in"].rearrange("(c p) d -> p c d", p=P)).then_inc(load["loaded"], 16)
                sp.dma_start(wx_nat[:, :], a["W_x"]).then_inc(load["loaded"], 16)
                sp.dma_start(wdt_nat[:, :, :], a["W_dt"].rearrange("(c p) r -> p c r", p=P)).then_inc(load["loaded"], 16)
                sp.dma_start(wo_nat[:, :], a["W_out"]).then_inc(load["loaded"], 16)
                sp.dma_start(conv_w[:, :, :], a["conv_w"].rearrange("(c p) o t -> p c (o t)", p=P)).then_inc(load["loaded"], 16)
                sp.dma_start(neg_a[:, :, :], a["A_log"].rearrange("(c p) n -> p c n", p=P)).then_inc(load["loaded"], 16)
                for i, v in enumerate((a["conv_b"], a["b_dt"], a["D"])):
                    sp.dma_start(vec_nat[:, i, :], v.rearrange("(c p) -> c p", p=P)).then_inc(load["loaded"], 16)

            @block.tensor
            def _(pe):
                pe.wait_ge(load["loaded"], 1 + 16 * 9)
                for c in range(4):
                    last = pe.transpose(psum[:, 0, c * P:(c + 1) * P], w_nat[:, c, :], k.ident[:, :])
                last.then_inc(load["turned"], 1)
                for c in range(CI):
                    pe.transpose(psum[:, 1, c * XD:(c + 1) * XD], wx_nat[:, c * P:(c + 1) * P], k.ident[0:XD, 0:XD])
                    pe.transpose(psum[0:DR, 2, c * P:(c + 1) * P], wdt_nat[:, c, :], k.ident[:, :])
                    last = pe.transpose(psum[:, 3, c * P:(c + 1) * P], wo_nat[:, c * P:(c + 1) * P], k.ident[:, :])
                for i in range(3):
                    last = pe.transpose(psum[:, 4, CI * i:CI * (i + 1)], vec_nat[:, i, :], k.ident[0:CI, 0:CI])
                last.then_inc(load["turned"], 1)

            @block.vector
            def _(dve):
                dve.wait_ge(load["turned"], 1 + 2)
                for i, t in enumerate((conv_b, b_dt, skip)):
                    dve.tensor_copy(t[:, :], psum[:, 4, CI * i:CI * (i + 1)])
                dve.tensor_copy(w_inT[:, :], psum[:, 0, :])
                dve.tensor_copy(w_xT[:, :, :], psum[:, 1, 0:CI * XD].rearrange("p (c x) -> p c x", c=CI))
                dve.tensor_copy(w_dtT[:, :], psum[0:DR, 2, 0:DI])
                dve.tensor_copy(w_outT[:, :, :], psum[:, 3, 0:DI].rearrange("p (c d) -> p c d", c=CI))
                dve.wait_ge(load["loaded"], 1 + 16 * 9)
                dve.tensor_scalar(neg_a[:, :, :], neg_a[:, :, :], 80.0, None, ALU.min).then_inc(load["copied"], 1)
                dve.wait_ge(load["done"], 1 + 1)
                dve.tensor_scalar(neg_a[:, :, :], neg_a[:, :, :], -1.0, None, ALU.mult)

            @block.scalar
            def _(act):
                act.wait_ge(load["copied"], 1 + 1)
                act.activation(neg_a[:, :, :], neg_a[:, :, :], ACT.Exp).then_inc(load["done"], 1)

            @block.gpsimd
            def _(pool):
                pool.memset(xd[:, :, :], 0.0)
                pool.memset(xp[:, :, :], 0.0)
                pool.memset(sel[:, :, :], 0.0).then_inc(s["zeroed"], 1)
                pool.wait_ge(s["zeroed"], 1 + 1)
                pool.affine_select(out=sel[:, :, :], in_=sel[:, :, :], compare_op=ALU.not_equal, fill=1.0, base=-DR,
                                   pattern=[[-1, 2 * DS], [0, P]], channel_multiplier=1).then_inc(s["sel"], 1)

        with nc.Block() as block:
            @block.tensor
            def _(pe):
                with pe.Fori(0, B) as b:
                    pe.wait_ge(s["xz_evac"], 1 + 4 * b) 
                    for c in range(4):
                        pe.matmul(psum[:, c, :], w_inT[:, c * P:(c + 1) * P], tokens(k.XA, b), start=True, stop=True).then_inc(s["xz_full"], 1)
                    pe.wait_ge(s["u_done"], 1 + CI * b + CI)
                    for c in range(CI):
                        last = pe.matmul(psum[0:XD, 4, :], w_xT[:, c, :], batch(u, c, b), start=(c == 0), stop=(c == CI - 1))
                    last.then_inc(s["xd_full"], 1)
                    pe.wait_ge(s["xd_evac"], 1 + b + 1)
                    for c in range(CI):
                        pe.matmul(psum[:, 5 + c, :], w_dtT[:, c * P:(c + 1) * P], dtr[:, :], start=True, stop=True).then_inc(s["dt_full"], 1)

            @block.vector
            def _(dve):
                with dve.Fori(0, B) as b:
                    for c in range(CI):
                        dve.wait_ge(s["xz_full"], 1 + 4 * b + c + 1)
                        dve.tensor_scalar(xp[:, c, DC - 1:DC - 1 + N], psum[:, c, :], 0.0, 1.0, ALU.max, ALU.min).then_inc(s["xz_evac"], 1)
                    for c in range(CI):
                        dve.wait_ge(s["xz_full"], 1 + 4 * b + CI + c + 1)
                        dve.tensor_scalar(batch(zb, c, b), psum[:, CI + c, :], 0.0, 1.0, ALU.max, ALU.min).then_inc(s["xz_evac"], 1)
                    for c in range(CI):
                        dve.wait_ge(s["xz_evac"], 1 + 4 * b + c + 1)
                        dve.tensor_scalar(conv[:, c, :], xp[:, c, 0:N], conv_w[:, c, 0:1], None, ALU.mult).then_inc(s["conv_step"], 1)
                        for t in range(1, DC):
                            dve.wait_ge(s["conv_step"], 1 + DC * (CI * b + c) + t)
                            dve.scalar_tensor_tensor(conv[:, c, :], xp[:, c, t:t + N], conv_w[:, c, t:t + 1], conv[:, c, :],
                                                     ALU.mult, ALU.add).then_inc(s["conv_step"], 1)
                    for c in range(CI):
                        dve.wait_ge(s["silu"], 1 + CI * b + c + 1)
                        dve.tensor_scalar(batch(u, c, b), conv[:, c, :], 0.0, 1.0, ALU.max, ALU.min).then_inc(s["u_done"], 1)
                    dve.wait_ge(s["xd_full"], 1 + b + 1)
                    dve.tensor_scalar(dtr[:, :], psum[0:DR, 4, :], 0.0, 1.0, ALU.max, ALU.min).then_inc(s["xd_evac"], 1)
                    for c in range(CI):
                        dve.wait_ge(s["dt_full"], 1 + CI * b + c + 1)
                        dve.tensor_scalar(conv[:, c, :], psum[:, 5 + c, :], b_dt[:, c:c + 1], None, ALU.add).then_inc(s["dt_in"], 1)
                        dve.wait_ge(s["dt_in"], 1 + CI * b + c + 1)
                        dve.scalar_tensor_tensor(tmp[:, c, :], conv[:, c, :], -1.0, conv[:, c, :], ALU.mult, ALU.min).then_inc(s["dt_abs"], 1)
                        dve.tensor_scalar(batch(dt, c, b), conv[:, c, :], 0.0, None, ALU.max).then_inc(s["dt_max"], 1)
                    for c in range(CI):
                        dve.wait_ge(s["dt_ln"], 1 + CI * b + c + 1)
                        dve.wait_ge(s["dt_max"], 1 + CI * b + c + 1)
                        dve.tensor_tensor(batch(dt, c, b), batch(dt, c, b), tmp[:, c, :], ALU.add).then_inc(s["dt_done"], 1)
                        dve.wait_ge(s["dt_done"], 1 + 2 * (CI * b + c) + 1)
                        dve.tensor_scalar(batch(dt, c, b), batch(dt, c, b), 1e-4, 20.0, ALU.max, ALU.min).then_inc(s["dt_done"], 1)

            @block.scalar
            def _(act):
                with act.Fori(0, B) as b:
                    for c in range(CI):
                        act.wait_ge(s["conv_step"], 1 + DC * (CI * b + c + 1))
                        act.activation(conv[:, c, :], conv[:, c, :], ACT.Silu, bias=conv_b[:, c:c + 1]).then_inc(s["silu"], 1)
                    wait_alone(act, s["xd_evac"], b + 1, s["scrap"])
                    act.activation(batch3(xd, b), psum[0:XD, 4, :], ACT.Copy).then_inc(s["copied"], 1)
                    for c in range(CI):
                        act.wait_ge(s["dt_abs"], 1 + CI * b + c + 1)
                        act.activation(tmp[:, c, :], tmp[:, c, :], ACT.Exp).then_inc(s["dt_exp"], 1)
                    for c in range(CI):
                        act.wait_ge(s["dt_exp"], 1 + CI * b + c + 1)
                        act.activation(tmp[:, c, :], tmp[:, c, :], ACT.Ln, bias=k.one[:, 0:1]).then_inc(s["dt_ln"], 1)
                for c in range(CI):
                    act.wait_ge(s["xz_evac"], 1 + 4 * B)
                    act.activation(zb[:, c, :, :], zb[:, c, :, :], ACT.Silu)

        with nc.Block() as block:
            @block.tensor
            def _(pe):
                with pe.Fori(0, B) as b:
                    def sums(n):
                        for c in range(CI):
                            pe.wait_ge(s["hc_done"], 1 + CI * DS * b + CI * n + c + 1)
                            if n == 0 and c == 0:
                                pe.wait_ge(s["y_evac"], 1 + CI * b)
                            pe.matmul(psum[:, 4 + c, :], k.ident[:, :], hc[:, (CI * n + c) % 4, :], start=(n == 0), stop=(n == DS - 1),
                                      skip_group_check=True).then_inc(s["y_full"], 1)

                    for n in range(DS):
                        if n >= 2:
                            pe.wait_ge(s["b_used"], 1 + CI * (DS * b + n - 1))
                            pe.wait_ge(s["c_copied"], 1 + DS * b + n - 1)
                        else:
                            pe.wait_ge(s["b_used"], 1 + CI * DS * b)
                            pe.wait_ge(s["c_copied"], 1 + DS * b)
                        for which in range(2):
                            pe.matmul(psum[:, 2 * which + n % 2, :], sel[:, DS * which + n, :], batch3(xd, b, P), start=True, stop=True).then_inc(s["bc_full"], 1)
                        if n >= 2:
                            sums(n - 2)
                    sums(DS - 2)
                    sums(DS - 1)
                    pe.wait_ge(s["yg_done"], 1 + CI * b + CI)
                    for c in range(CI):
                        last = pe.matmul(psum[:, 6, :], w_outT[:, c, :], yg[:, c, :], start=(c == 0), stop=(c == CI - 1))
                    last.then_inc(s["out_full"], 1)

            @block.scalar
            def _(act):
                with act.Fori(0, B) as b:
                    for n in range(DS):
                        m0 = CI * (DS * b + n)
                        for c in range(CI):
                            wait_alone(act, s["scanned"], m0 + c - 3 if CI * n + c >= 4 else CI * DS * b, s["scrap"])
                            act.activation(da[:, (CI * n + c) % 4, :], batch(dt, c, b), ACT.Exp, scale=neg_a[:, c, n:n + 1]).then_inc(s["da_done"], 1)
                        act.wait_ge(s["bc_full"], 1 + 2 * (DS * b + n) + 2)
                        if n >= 2:
                            act.wait_ge(s["hc_done"], 1 + m0 - 2)
                        else:
                            act.wait_ge(s["hc_done"], 1 + CI * DS * b)
                        act.activation(c_sb[:, n % 2, :], psum[:, 2 + n % 2, :], ACT.Copy).then_inc(s["c_copied"], 1)

            @block.vector
            def _(dve):
                with dve.Fori(0, B) as b:
                    for c in range(CI):
                        dve.tensor_tensor(dtu[:, c, :], batch(dt, c, b), batch(u, c, b), ALU.mult).then_inc(s["staged"], 1)
                    dve.wait_ge(s["staged"], 1 + CI * b + CI)
                    for n in range(DS):
                        for c in range(CI):
                            i = CI * n + c
                            m = CI * DS * b + i
                            dve.wait_ge(s["bc_full"], 1 + 2 * (DS * b + n) + 1)
                            dve.tensor_tensor(dbu[:, i % 4, :], dtu[:, c, :], psum[:, n % 2, :], ALU.mult).then_inc(s["b_used"], 1)
                            dve.wait_ge(s["b_used"], 1 + m + 1)
                            dve.wait_ge(s["da_done"], 1 + m + 1)
                            if i >= 4:
                                dve.wait_ge(s["hc_done"], 1 + m - 3)
                            dve.tensor_tensor_scan(hs[:, i % 4, :], da[:, i % 4, :], dbu[:, i % 4, :], 0.0, ALU.mult, ALU.add).then_inc(s["scanned"], 1)
                    for c in range(CI):
                        dve.wait_ge(s["y_full"], 1 + CI * DS * b + CI * (DS - 1) + c + 1)
                        dve.scalar_tensor_tensor(tmp[:, c, :], batch(u, c, b), skip[:, c:c + 1], psum[:, 4 + c, :], ALU.mult, ALU.add).then_inc(s["y_evac"], 1)
                        dve.wait_ge(s["y_evac"], 1 + CI * b + c + 1)
                        dve.tensor_scalar(tmp[:, c, :], tmp[:, c, :], 0.0, 1.0, ALU.max, ALU.min).then_inc(s["y_step"], 1)
                        dve.wait_ge(s["y_step"], 1 + 2 * (CI * b + c) + 1)
                        dve.tensor_tensor(tmp[:, c, :], tmp[:, c, :], batch(zb, c, b), ALU.mult).then_inc(s["y_step"], 1)
                        dve.wait_ge(s["y_step"], 1 + 2 * (CI * b + c) + 2)
                        dve.tensor_scalar(yg[:, c, :], tmp[:, c, :], 0.0, 1.0, ALU.max, ALU.min).then_inc(s["yg_done"], 1)
                    dve.wait_ge(s["out_full"], 1 + b + 1)
                    dve.tensor_tensor(tokens(k.X, b), tokens(k.X, b), psum[:, 6, :], ALU.add).then_inc(s["out_done"], 1)

            @block.gpsimd
            def _(pool):
                with pool.Fori(0, B) as b:
                    for n in range(DS):
                        for c in range(CI):
                            i = CI * n + c
                            m = CI * DS * b + i
                            pool.wait_ge(s["scanned"], 1 + m + 1)
                            pool.wait_ge(s["c_copied"], 1 + DS * b + n + 1)
                            if i >= 4:
                                pool.wait_ge(s["y_full"], 1 + m - 3)
                            else:
                                pool.wait_ge(s["y_full"], 1 + CI * DS * b)
                            pool.tensor_tensor(hc[:, i % 4, :], hs[:, i % 4, :], c_sb[:, n % 2, :], ALU.mult).then_inc(s["hc_done"], 1)


def tokens(x, b):
    return x[:, ds(b, 1), PAD:ROW].rearrange("p o n -> p (o n)")


def batch(x, c, b):
    return x[:, c, ds(b, 1), :].rearrange("p o n -> p (o n)")


def batch3(x, b, rows=XD):
    return x[0:rows, ds(b, 1), :].rearrange("p o n -> p (o n)")



KEYS = MEM + N


def topk_phase(k, a):
    nc = k.nc
    psum = k.psum
    with ExitStack() as ctx:
        s = names(ctx, "tk", nc, "w_in", "mem_turned", "mem_copied", "scaled", "staged", "proj_full", "proj_evac", "qs_done", "dots", "copied", "added", "m8", "removed",
                  "neg_top", "e_done", "p_done", "pt_full", "pt_evac", "pv_full", "rden", "o_done", "ot_full", "ot_evac", "y_full", "y_done", "scrap")

        def sb(name, shape, dt=F32):
            return ctx.enter_context(nc.sbuf_tensor(f"tk_{name}", shape, dt))

        wq = sb("wq", [P, INNER])
        wkv = sb("wkv", [P, 2 * INNER])
        wout = sb("wout", [P, PAIRS, D])
        bout = sb("bout", [P, 1])
        mix = sb("mix", [P, PAIRS, H])
        mk = sb("mk", [MEM, H, DH])
        mkT = sb("mkT", [P, PAIRS, MEM])
        mixed_mk = sb("mixed_mk", [P, PAIRS, H, MEM])
        hb = sb("hb", [P, N])
        qT = sb("qT", [P, PAIRS, N])
        kT = sb("kT", [P, PAIRS, N])
        v = sb("v", [P, TILES, H, DH + 1])
        mv = sb("mv", [MEM, H, DH + 1])
        qs = sb("qs", [P, 2, PAIRS, P])
        scores = sb("scores", [P, 2, 2, KEYS])
        work = sb("work", [P, 2, KEYS])
        m8 = sb("m8", [P, 2, TOPK])
        neg_top = sb("neg_top", [P, 2, 1])
        e = sb("e", [P, 2, KEYS])
        pT = sb("pT", [P, 2, TILES + 1, P])
        rden = sb("rden", [P, 2, 1])
        o_tok = sb("o_tok", [P, H, DH])
        oT = sb("oT", [P, PAIRS, P])
        y = sb("y", [P, P])

        ROUNDS = TOPK // 8

        with nc.Block() as block:
            @block.sync
            def _(sp):
                sp.dma_start(wq[:, :], a["Wq"]).then_inc(s["w_in"], 16)
                sp.dma_start(wkv[:, :], a["Wkv"]).then_inc(s["w_in"], 16)
                sp.dma_start(wout[:, :, :], a["Wout"].rearrange("(c p) d -> p c d", p=P)).then_inc(s["w_in"], 16)
                sp.dma_start(bout[:, :], a["bout"].rearrange("(p o) -> p o", o=1), allow_slow_non_contiguous=True).then_inc(s["w_in"], 16)
                pre = a["pre_proj"].rearrange("(c r) k -> r c k", r=2)
                for r in range(2):
                    sp.dma_start(mix[DH * r:DH * (r + 1), :, :], pre[r, :, :].partition_broadcast(DH)).then_inc(s["w_in"], 16)
                sp.dma_start(mk[:, :, :], a["mem_k"].rearrange("h m e -> m h e")).then_inc(s["w_in"], 16)
                sp.dma_start(mv[:, :, 0:DH], a["mem_v"].rearrange("h m e -> m h e")).then_inc(s["w_in"], 16)

            @block.tensor
            def _(pe):
                pe.wait_ge(s["w_in"], 1 + 16 * 8)
                for c in range(PAIRS):
                    last = pe.transpose(psum[:, 0, MEM * c:MEM * (c + 1)], mk[:, 2 * c:2 * c + 2, :].rearrange("m h e -> m (h e)"),
                                        k.ident[0:MEM, 0:MEM])
                last.then_inc(s["mem_turned"], 1)

            @block.vector
            def _(dve):
                dve.wait_ge(s["w_in"], 1 + 16 * 8)
                dve.tensor_scalar(mix[:, :, :], mix[:, :, :], DH ** -0.5, None, ALU.mult).then_inc(s["scaled"], 1)
                dve.memset(v[:, :, :, DH:DH + 1], 1.0)
                dve.memset(mv[:, :, DH:DH + 1], 1.0)
                dve.wait_ge(s["mem_turned"], 1 + 1)
                dve.tensor_copy(mkT[:, :, :], psum[:, 0, 0:MEM * PAIRS].rearrange("p (c m) -> p c m", m=MEM)).then_inc(s["mem_copied"], 1)
                dve.wait_ge(s["scaled"], 1 + 1)
                dve.wait_ge(s["mem_copied"], 1 + 1)
                for c in range(PAIRS):
                    dve.tensor_tensor(mixed_mk[:, c, :, :], mix[:, c, :].unsqueeze(2).to_broadcast([P, H, MEM]),
                                      mkT[:, c, :].unsqueeze(1).to_broadcast([P, H, MEM]), ALU.mult)

        UNITS = H * TILES
        ORDER = (3, 2, 1, 0)
        QK_UNITS, V_UNITS = 4, 2
        TILE_UNITS = QK_UNITS + V_UNITS

        def tile_at(pos):
            return ORDER[pos % TILES]

        def unit(b, pos, p, j):
            return UNITS * b + H * pos + 2 * p + j

        def heads(p, j):
            return slice(2 * p + j, 2 * p + j + 1) if isinstance(p, int) else ds(2 * p + j, 1)

        def flat(x):
            return x.rearrange("p o e -> p (o e)")

        def proj_bank(n):
            return 3 if n % 2 == 0 else 5

        with nc.Block() as block:
            @block.tensor
            def _(pe):
                def project_qk(b, pos):
                    t = tile_at(pos)
                    first = 3 * 8 * b + TILE_UNITS * pos
                    for n in range(QK_UNITS):
                        pe.wait_ge(s["proj_evac"], 1 + first + n + 1)
                        w, w0 = (wq, 512 * n) if n < 2 else (wkv, 512 * (n - 2))
                        for c in range(4):
                            last = pe.matmul(psum[:, proj_bank(n), P * c:P * (c + 1)], w[:, w0 + P * c:w0 + P * (c + 1)], hb[:, P * t:P * (t + 1)],
                                             start=True, stop=True)
                        last.then_inc(s["proj_full"], 1)

                def project_v(b, pos):
                    t = tile_at(pos)
                    first = 3 * 8 * b + TILE_UNITS * pos + QK_UNITS
                    for n in range(V_UNITS):
                        pe.wait_ge(s["proj_evac"], 1 + first + n + 1)
                        pe.matmul(psum[:, proj_bank(n), :], hb[:, P * t:P * (t + 1)], wkv[:, INNER + 512 * n:INNER + 512 * (n + 1)],
                                  start=True, stop=True).then_inc(s["proj_full"], 1)

                def projected(b, pos, units):
                    pe.wait_ge(s["proj_evac"], 1 + 3 * 8 * b + TILE_UNITS * pos + units + 2)

                def dots(b, pos, p):
                    t = tile_at(pos)
                    n = P * (t + 1)
                    for j in range(2):
                        g = unit(b, pos, p, j)
                        start = isinstance(b, int)
                        if isinstance(p, int) and p == 0 and j == 0:
                            if not start:
                                pe.wait_ge(s["copied"], 1 + unit(b, pos, 0, 0))
                            for c in range(PAIRS):
                                pe.matmul(psum[:, 2, 0:H * MEM], qT[:, c, P * t:P * (t + 1)], mixed_mk[:, c, :, :].rearrange("p h m -> p (h m)"),
                                          start=(c == 0), stop=(c == PAIRS - 1))
                        pe.wait_ge(s["qs_done"], 1 + g + 1)
                        if not start:
                            pe.wait_ge(s["copied"], 1 + g - 1)
                        for c in range(PAIRS):
                            pe.matmul(psum[:, j, 0:n], qs[:, j, c, :], kT[:, c, 0:n], start=(c == 0), stop=False, skip_group_check=True)
                        pe.matmul(psum[:, j, n - P:n], k.ident_bf[:, :], k.causal[:, :], start=False, stop=True,
                                  skip_group_check=True).then_inc(s["dots"], 1)

                def values(b, pos, p):
                    t = tile_at(pos)
                    for j in range(2):
                        g = unit(b, pos, p, j)
                        pe.wait_ge(s["p_done"], 1 + g + 1)
                        pe.wait_ge(s["pt_evac"], 1 + g)
                        for i in range(t + 2):
                            lo, m = (0, MEM) if i == 0 else (MEM + P * (i - 1), P)
                            last = pe.transpose(psum[0:m, 4 + i // 4, P * (i % 4):P * (i % 4 + 1)], e[:, j, lo:lo + m], k.ident[:, :])
                        last.then_inc(s["pt_full"], 1)
                    for j in range(2):
                        g = unit(b, pos, p, j)
                        pe.wait_ge(s["pt_evac"], 1 + g + 1)
                        if pos == 0 and isinstance(p, int) and p == 0:
                            pe.wait_ge(s["o_done"], 1 + unit(b, 0, 0, 0))
                        else:
                            pe.wait_ge(s["o_done"], 1 + g - 1)
                        for i in range(t + 2):
                            src = mv[:, heads(p, j), :] if i == 0 else v[:, i - 1, heads(p, j), :]
                            last = pe.matmul(psum[:, 6 + j, 0:DH + 1], pT[0:(MEM if i == 0 else P), j, i, :], flat(src), start=(i == 0), stop=(i == t + 1))
                        last.then_inc(s["pv_full"], 1)

                def output(b, pos):
                    pe.wait_ge(s["o_done"], 1 + unit(b, pos + 1, 0, 0))
                    for half in range(2):
                        for c in range(4):
                            hh = 8 * half + 2 * c
                            last = pe.transpose(psum[:, 4 + half, P * c:P * (c + 1)], o_tok[:, hh:hh + 2, :].rearrange("p h e -> p (h e)"), k.ident[:, :])
                        last.then_inc(s["ot_full"], 1)
                    pe.wait_ge(s["ot_evac"], 1 + 2 * (TILES * b + pos) + 2)
                    for c in range(PAIRS):
                        last = pe.matmul(psum[:, 2, H * MEM:H * MEM + P], wout[:, c, :], oT[:, c, :], start=(c == 0), stop=(c == PAIRS - 1))
                    last.then_inc(s["y_full"], 1)

                pe.wait_ge(s["staged"], 1 + 1)
                for pos in range(TILES):
                    project_qk(0, pos)
                    if pos < TILES - 1:
                        project_v(0, pos)
                projected(0, TILES - 1, QK_UNITS)
                dots(0, 0, 0)
                with pe.Fori(0, B) as b:
                    for pos in range(TILES):
                        dots(b, pos, 1)
                        if pos == 0:
                            project_v(b, TILES - 1)
                            projected(b, TILES, 0)
                        else:
                            project_v(b + 1, pos - 1)
                            projected(b + 1, pos, 0)
                            output(b, pos - 1)
                        values(b, pos, 0)
                        with pe.Fori(1, PAIRS - 2) as p:
                            dots(b, pos, p + 1)
                            values(b, pos, p)
                        dots(b, pos, PAIRS - 1)
                        if pos == 0:
                            pe.wait_ge(s["staged"], 1 + b + 2)
                        project_qk(b + 1, pos)
                        projected(b + 1, pos, QK_UNITS)
                        values(b, pos, PAIRS - 2)
                        dots(b, pos + 1, 0)
                        values(b, pos, PAIRS - 1)
                    output(b, TILES - 1)

            @block.scalar
            def _(act):
                def copy_qk(b, pos):
                    t = tile_at(pos)
                    for n in range(QK_UNITS):
                        act.wait_ge(s["proj_full"], 1 + 3 * 8 * b + TILE_UNITS * pos + n + 1)
                        dst = qT if n < 2 else kT
                        act.activation(dst[:, 4 * (n % 2):4 * (n % 2) + 4, P * t:P * (t + 1)], psum[:, proj_bank(n), :].rearrange("p (c t) -> p c t", t=P),
                                       ACT.Copy).then_inc(s["proj_evac"], 1)

                def copy_v(b, pos):
                    t = tile_at(pos)
                    for n in range(V_UNITS):
                        act.wait_ge(s["proj_full"], 1 + 3 * 8 * b + TILE_UNITS * pos + QK_UNITS + n + 1)
                        act.activation(v[:, t, 8 * n:8 * n + 8, 0:DH], psum[:, proj_bank(n), :].rearrange("p (h e) -> p h e", e=DH), ACT.Copy).then_inc(s["proj_evac"], 1)

                def copy_scores(b, pos, p, parity):
                    n = P * (tile_at(pos) + 1)
                    for j in range(2):
                        act.wait_ge(s["dots"], 1 + unit(b, pos, p, j) + 1)
                        act.activation(scores[:, parity, j, MEM:MEM + n], psum[:, j, 0:n], ACT.Copy)
                        memory = psum[:, 2, 0:H * MEM].rearrange("p (h m) -> p h m", m=MEM)[:, heads(p, j), :]
                        act.activation(scores[:, parity, j, 0:MEM], flat(memory), ACT.Copy).then_inc(s["copied"], 1)

                def exps(b, pos, p, parity):
                    n = MEM + P * (tile_at(pos) + 1)
                    for j in range(2):
                        act.wait_ge(s["neg_top"], 1 + unit(b, pos, p, j) + 1)
                        act.activation(e[:, j, 0:n], scores[:, parity, j, 0:n], ACT.Exp, bias=neg_top[:, j, :]).then_inc(s["e_done"], 1)

                def copy_turned(b, pos, p):
                    t = tile_at(pos)
                    for j in range(2):
                        act.wait_ge(s["pt_full"], 1 + unit(b, pos, p, j) + 1)
                        act.activation(pT[0:MEM, j, 0, :], psum[0:MEM, 4, 0:P], ACT.Copy)
                        last = act.activation(pT[:, j, 1:min(t + 2, 4), :], psum[:, 4, P:P * min(t + 2, 4)].rearrange("p (i n) -> p i n", n=P), ACT.Copy)
                        if t == 3:
                            last = act.activation(pT[:, j, 4, :], psum[:, 5, 0:P], ACT.Copy)
                        last.then_inc(s["pt_evac"], 1)

                def outputs(b, pos, p):
                    for j in range(2):
                        wait_alone(act, s["rden"], unit(b, pos, p, j) + 1, s["scrap"])
                        act.activation(flat(o_tok[:, heads(p, j), :]), psum[:, 6 + j, 0:DH], ACT.Copy, scale=rden[:, j, :]).then_inc(s["o_done"], 1)

                def copy_ot(b, pos):
                    for half in range(2):
                        act.wait_ge(s["ot_full"], 1 + 2 * (TILES * b + pos) + half + 1)
                        act.activation(oT[:, 4 * half:4 * half + 4, :].rearrange("p c t -> p (c t)"), psum[:, 4 + half, :], ACT.Copy).then_inc(s["ot_evac"], 1)

                def copy_y(b, pos):
                    act.wait_ge(s["y_full"], 1 + TILES * b + pos + 1)
                    act.wait_ge(s["added"], 1 + TILES * b + pos)
                    act.activation(y[:, :], psum[:, 2, H * MEM:H * MEM + P], ACT.Identity, bias=bout[:, 0:1]).then_inc(s["y_done"], 1)

                act.sem_inc(s["proj_evac"], 2)
                for pos in range(TILES):
                    copy_qk(0, pos)
                    if pos < TILES - 1:
                        copy_v(0, pos)
                copy_scores(0, 0, 0, 0)
                with act.Fori(0, B) as b:
                    exps(b, 0, 0, 0)
                    for pos in range(TILES):
                        copy_scores(b, pos, 1, 1)
                        if pos == 0:
                            copy_v(b, TILES - 1)
                        else:
                            copy_v(b + 1, pos - 1)
                            copy_ot(b, pos - 1)
                        copy_turned(b, pos, 0)
                        exps(b, pos, 1, 1)
                        if pos:
                            copy_y(b, pos - 1)
                        outputs(b, pos, 0)
                        with act.Fori(0, 2) as q:
                            for p, parity in ((2 * q + 1, 0), (2 * q + 2, 1)):
                                copy_scores(b, pos, p + 1, parity)
                                copy_turned(b, pos, p)
                                exps(b, pos, p + 1, parity)
                                outputs(b, pos, p)
                        for p, parity in ((5, 0), (6, 1)):
                            copy_scores(b, pos, p + 1, parity)
                            if p == 6:
                                copy_qk(b + 1, pos)
                            copy_turned(b, pos, p)
                            exps(b, pos, p + 1, parity)
                            outputs(b, pos, p)
                        copy_scores(b, pos + 1, 0, 0)
                        copy_turned(b, pos, PAIRS - 1)
                        if pos < TILES - 1:
                            exps(b, pos + 1, 0, 0)
                        outputs(b, pos, PAIRS - 1)
                    copy_ot(b, TILES - 1)
                    copy_y(b, TILES - 1)

            @block.vector
            def _(dve):
                def recip(b, pos, p, j):
                    dve.wait_ge(s["pv_full"], 1 + unit(b, pos, p, j) + 1)
                    dve.reciprocal(rden[:, j, :], psum[:, 6 + j, DH:DH + 1]).then_inc(s["rden"], 1)

                def pair(b, pos, p, parity, between):
                    n = MEM + P * (tile_at(pos) + 1)
                    g = unit(b, pos, p, 0)
                    found, gone = ROUNDS * g, (ROUNDS - 1) * g
                    for r in range(ROUNDS):
                        def src(j):
                            return work[:, j, 0:n] if r else scores[:, parity, j, 0:n]

                        for j in range(2):
                            if r:
                                wait_alone(dve, s["removed"], gone + 2 * (r - 1) + j + 1, s["scrap"])
                            else:
                                wait_alone(dve, s["copied"], g + j + 1, s["scrap"])
                            dve.max(m8[:, j, 8 * r:8 * r + 8], src(j)).then_inc(s["m8"], 1)
                        for j in range(2):
                            wait_alone(dve, s["m8"], found + 2 * r + j + 1, s["scrap"])
                            if r == 0:
                                dve.tensor_scalar(neg_top[:, j, :], m8[:, j, 0:1], -1.0, None, ALU.mult).then_inc(s["neg_top"], 1)
                            if r < ROUNDS - 1:
                                dve.match_replace(work[:, j, 0:n], m8[:, j, 8 * r:8 * r + 8], src(j), REMOVED).then_inc(s["removed"], 1)
                        if r in between:
                            between[r]()
                    for j in range(2):
                        dve.wait_ge(s["e_done"], 1 + g + j + 1)
                        dve.scalar_tensor_tensor(e[:, j, 0:n], scores[:, parity, j, 0:n], m8[:, j, TOPK - 1:TOPK], e[:, j, 0:n],
                                                 ALU.is_ge, ALU.mult).then_inc(s["p_done"], 1)

                def stage(b):
                    dve.wait_ge(s["proj_full"], 1 + 3 * 8 * b)
                    dve.tensor_copy(hb[:, :], tokens(k.XA, b)).then_inc(s["staged"], 1)

                def recips(b, pos, p):
                    return {3: lambda: recip(b, pos, p, 0), 5: lambda: recip(b, pos, p, 1)}

                dve.tensor_copy(hb[:, :], k.XA[:, 0, PAD:ROW]).then_inc(s["staged"], 1)
                with dve.Fori(0, B) as b:
                    for pos in range(TILES):
                        pair(b, pos, 0, 0, recips(b, pos - 1, PAIRS - 1) if pos else {})
                        between = recips(b, pos, 0)
                        if pos == 0:
                            between[2] = lambda: stage(b + 1)
                        pair(b, pos, 1, 1, between)
                        with dve.Fori(1, PAIRS // 2) as q:
                            pair(b, pos, 2 * q, 0, recips(b, pos, 2 * q - 1))
                            pair(b, pos, 2 * q + 1, 1, recips(b, pos, 2 * q))
                    for j in range(2):
                        recip(b, TILES - 1, PAIRS - 1, j)

            @block.gpsimd
            def _(pool):
                def scale(b, pos, p):
                    t = tile_at(pos)
                    for j in range(2):
                        if not isinstance(b, int):
                            pool.wait_ge(s["dots"], 1 + unit(b, pos, p, j) - 1)
                        pool.tensor_tensor(qs[:, j, :, :], qT[:, :, P * t:P * (t + 1)], mix[:, :, heads(p, j)].to_broadcast([P, PAIRS, P]),
                                           ALU.mult).then_inc(s["qs_done"], 1)

                def add_y(b, pos):
                    t = tile_at(pos)
                    pool.wait_ge(s["y_done"], 1 + TILES * b + pos + 1)
                    xt = k.X[:, ds(b, 1), PAD + P * t:PAD + P * (t + 1)].rearrange("p o n -> p (o n)")
                    pool.tensor_tensor(xt, y[:, :], xt, ALU.add).then_inc(s["added"], 1)

                pool.wait_ge(s["proj_evac"], 1 + 3 * 8 - V_UNITS + 2)
                scale(0, 0, 0)
                with pool.Fori(0, B) as b:
                    for pos in range(TILES):
                        scale(b, pos, 1)
                        scale(b, pos, 2)
                        if pos:
                            add_y(b, pos - 1)
                        with pool.Fori(3, PAIRS) as p:
                            scale(b, pos, p)
                        if pos == TILES - 1:
                            pool.wait_ge(s["proj_evac"], 1 + 3 * 8 * (b + 1) + 3 * 8 - V_UNITS + 2)
                        scale(b, pos + 1, 0)
                    add_y(b, TILES - 1)



def build(nc, a, out):
    with ExitStack() as ctx:
        def sb(name, shape, dt=F32):
            return ctx.enter_context(nc.sbuf_tensor(name, shape, dt))

        k = Kit()
        k.nc = nc
        k.psum = ctx.enter_context(nc.psum_tensor("psum", [P, 8, 512], F32))
        k.X, k.XB = (sb(name, [P, B, ROW]) for name in ("X", "XB"))
        k.XA = sb("XA", [P, B + 1, ROW])
        k.ident, k.ident_bf, k.mean_w = sb("ident", [P, P]), sb("ident_bf", [P, P], BF16), sb("mean_w", [P, P])
        k.row_w = sb("row_w", [P, TILES, P])
        k.mask_f, k.causal, k.band = sb("mask_f", [P, P]), sb("causal", [P, P], BF16), sb("band", [P, 2, 8, 2 * WIN], BF16)
        k.eps, k.one, k.magic = sb("eps", [P, 1]), sb("one", [P, 1]), sb("magic", [P, 2 * H], U32)
        k.b1, k.b2 = sb("b1", [P, DEPTH, 2, 3]), sb("b2", [P, DEPTH])
        k.ln_g, k.ln_b = sb("ln_g", [P, DEPTH]), sb("ln_b", [P, DEPTH])
        k.rot_base, k.qk_gain = sb("rot_base", [P, 4, TILES, DH]), sb("qk_gain", [P, 2, DEPTH, DH])
        load_phase(k, a)
        norm_phase(k, "n0")
        mamba_phase(k, a)
        norm_phase(k, "n1")
        ffn_stack(k, a, "f0")
        add_phase(k, "a0")
        norm_phase(k, "n2")
        topk_phase(k, a)
        norm_phase(k, "n3")
        ffn_stack(k, a, "f1")
        add_phase(k, "a1")
        store_phase(k, out)


_INS = {"x": "L0_attn_a_hidden_states", "W_in": "L0_attn_a_W_in", "conv_w": "L0_attn_a_conv_w", "conv_b": "L0_attn_a_conv_b",
        "W_x": "L0_attn_a_W_x", "W_dt": "L0_attn_a_W_dt", "b_dt": "L0_attn_a_b_dt", "W_out": "L0_attn_a_W_out",
        "A_log": "L0_attn_a_A_log", "D": "L0_attn_a_D", "Wq": "L0_attn_b_Wq", "Wkv": "L0_attn_b_Wkv",
        "pre_proj": "L0_attn_b_pre_proj", "mem_k": "L0_attn_b_mem_k", "mem_v": "L0_attn_b_mem_v", "Wout": "L0_attn_b_Wout",
        "bout": "L0_attn_b_bout", "Wqkv": "L0_ffn_Wqkv", "q_scale": "L0_ffn_q_scale", "k_scale": "L0_ffn_k_scale", "Wo": "L0_ffn_Wo",
        "ln_g": "L0_ffn_ln_g", "ln_b": "L0_ffn_ln_b", "W1": "L0_ffn_W1", "b1": "L0_ffn_b1", "W2": "L0_ffn_W2", "b2": "L0_ffn_b2"}


def kernel(**inputs):
    import concourse.bacc as bacc
    from concourse.bass_utils import run_bass_kernel_spmd

    nc = bacc.Bacc("TRN2", target_bir_lowering=False, num_devices=1)
    arrays, args = {}, {}
    for name, given in _INS.items():
        arrays[f"in_{name}"] = np.ascontiguousarray(inputs[given])
    arrays["in_rot"] = rotary_tables()
    for key, v in arrays.items():
        args[key[3:]] = nc.dram_tensor(key, v.shape, mybir.dt.from_np(v.dtype), kind="ExternalInput").ap()
    out = nc.dram_tensor("out", (B, N, D), F32, kind="ExternalOutput").ap()
    build(nc, args, out)
    r = run_bass_kernel_spmd(nc, [arrays], core_ids=[0])
    return r.results[0]["out"]
```
